# Optimizing a Trainium2 kernel written in Bass

```python
import numpy as np
import jax
import jax.numpy as jnp

def _softmax(x, axis=-1):
    return jax.nn.softmax(x, axis=axis)

def _gelu(x):
    return jax.nn.gelu(x, approximate=True)

def _silu(x):
    return jax.nn.silu(x)

def _sigmoid(x):
    return jax.nn.sigmoid(x)

def _layernorm(x, axis=-1, eps=1e-05):
    m = jnp.mean(x, axis=axis, keepdims=True)
    v = jnp.var(x, axis=axis, keepdims=True)
    return (x - m) / jnp.sqrt(v + eps)

def _scatter_add(tgt, idx, src, axis=0):
    return tgt.at[idx].add(src)

def _segment_sum(src, seg, n):
    return jax.ops.segment_sum(src, seg, n)
kernel_name = 'mk_adj_preln_d2_adj_r2_4ad4a1'

def setup_inputs(seed: int=0):
    np.random.seed(seed)
    _w = jnp.asarray

    def _rec_inputs():
        import jax
        import jax.numpy as jnp
        _gk = jax.random.key(seed)
        x = -0.0001538 + 1 * jax.random.normal(jax.random.fold_in(_gk, 1), (16, 512, 384), jnp.float32)
        _w = (1.0 + jnp.arange(512, dtype=jnp.float32)) ** (-0.5)
        _w = _w / _w.mean()
        _pij = jnp.clip(0.015625 * _w[:, None] * _w[None, :], 0.0, 1.0)
        _a = jax.random.uniform(jax.random.fold_in(_gk, 2), (16, 512, 512)) < _pij
        _af = _a.astype(jnp.float32)
        adj = _af
        return (x, adj)
    x, adj = _rec_inputs()

    def _L0_gnn_setup():
        import jax, jax.numpy as jnp
        import numpy as np
        LN_EPS = 1e-12

        def _digcn_forward(hidden_state, adjacency_matrix, Wl, bl, Ws, bs, Wr, br, ln_w, ln_b):
            B, S, D = hidden_state.shape
            temper = jnp.asarray(D, jnp.float32) ** 0.5
            i = jnp.arange(S)
            upper = (i[None, :] > i[:, None]).astype(hidden_state.dtype)
            lower = (i[None, :] < i[:, None]).astype(hidden_state.dtype)

            def layer(h, params):
                wl, b_l, ws, b_s, wr, b_r, g, beta = params
                u = jnp.einsum('bid,bjd->bij', h, h) / temper
                a = jax.nn.softmax(u, axis=-1)
                delta = a * adjacency_matrix
                attn = delta / (jnp.sum(delta, axis=-1, keepdims=True) + 1e-10)
                hl = h @ wl.T + b_l
                hs = h @ ws.T + b_s
                hr = h @ wr.T + b_r
                diag_a = jnp.diagonal(attn, axis1=1, axis2=2)
                ctx = jnp.einsum('bij,bjd->bid', attn * upper, hl) + diag_a[..., None] * hs + jnp.einsum('bij,bjd->bid', attn * lower, hr)
                mean = ctx.mean(-1, keepdims=True)
                var = ctx.var(-1, keepdims=True)
                o = (ctx - mean) / jnp.sqrt(var + LN_EPS) * g + beta
                return (jax.nn.relu(o), None)
            out, _ = jax.lax.scan(layer, hidden_state, (Wl, bl, Ws, bs, Wr, br, ln_w, ln_b))
            return out
        key = jax.random.key(seed)
        ks = jax.random.split(key, 6)
        B, S, D, L = (8, 512, 384, 2)
        scale = (1.0 / D) ** 0.5
        hidden_state = jax.random.normal(ks[0], (B, S, D), jnp.float32)
        adjacency_matrix = (jax.random.uniform(ks[1], (B, S, S)) < 0.05).astype(jnp.float32)
        Wl = jax.random.normal(ks[2], (L, D, D), jnp.float32) * scale
        Ws = jax.random.normal(ks[3], (L, D, D), jnp.float32) * scale
        Wr = jax.random.normal(ks[4], (L, D, D), jnp.float32) * scale
        bl = jnp.zeros((L, D), jnp.float32)
        bs = jnp.zeros((L, D), jnp.float32)
        br = jnp.zeros((L, D), jnp.float32)
        ln_w = jnp.ones((L, D), jnp.float32)
        ln_b = jnp.zeros((L, D), jnp.float32)
        return dict(hidden_state=hidden_state, adjacency_matrix=adjacency_matrix, Wl=Wl, bl=bl, Ws=Ws, bs=bs, Wr=Wr, br=br, ln_w=ln_w, ln_b=ln_b)
    _L0_gnn_all = _L0_gnn_setup()
    _L0_gnn_in = {k: v for k, v in _L0_gnn_all.items() if k in ('Wl', 'bl', 'Ws', 'bs', 'Wr', 'br', 'ln_w', 'ln_b')}
    del _L0_gnn_all

    def _L1_gnn_setup():
        import jax, jax.numpy as jnp
        import numpy as np
        B, S, H, L = (32, 256, 384, 2)

        def _layer_norm(z, a, b, eps=0.001):
            mu = jnp.mean(z, axis=-1, keepdims=True)
            sigma = jnp.std(z, axis=-1, keepdims=True, ddof=1)
            return (z - mu) / (sigma + eps) * a + b
        key = jax.random.key(seed)
        ks = jax.random.split(key, 6)
        hidden_state = jax.random.normal(ks[0], (B, S, H), dtype=jnp.float32)
        adjacency_matrix = (jax.random.uniform(ks[1], (B, S, S)) < 0.2).astype(jnp.float32)
        W_left = 0.05 * jax.random.normal(ks[2], (L, H, H), dtype=jnp.float32)
        W_right = 0.05 * jax.random.normal(ks[3], (L, H, H), dtype=jnp.float32)
        W_lin = 0.05 * jax.random.normal(ks[4], (L, H, H), dtype=jnp.float32)
        b_lin = jnp.zeros((L, H), dtype=jnp.float32)
        ln_a = jnp.ones((L, H), dtype=jnp.float32)
        ln_b = jnp.zeros((L, H), dtype=jnp.float32)
        return {'hidden_state': hidden_state, 'adjacency_matrix': adjacency_matrix, 'W_left': W_left, 'W_right': W_right, 'W_lin': W_lin, 'b_lin': b_lin, 'ln_a': ln_a, 'ln_b': ln_b}
    _L1_gnn_all = _L1_gnn_setup()
    _L1_gnn_in = {k: v for k, v in _L1_gnn_all.items() if k in ('W_left', 'W_right', 'W_lin', 'b_lin', 'ln_a', 'ln_b')}
    del _L1_gnn_all
    return {'x': x, 'adj': adj, 'L0_gnn_Wl': _L0_gnn_in['Wl'], 'L0_gnn_bl': _L0_gnn_in['bl'], 'L0_gnn_Ws': _L0_gnn_in['Ws'], 'L0_gnn_bs': _L0_gnn_in['bs'], 'L0_gnn_Wr': _L0_gnn_in['Wr'], 'L0_gnn_br': _L0_gnn_in['br'], 'L0_gnn_ln_w': _L0_gnn_in['ln_w'], 'L0_gnn_ln_b': _L0_gnn_in['ln_b'], 'L1_gnn_W_left': _L1_gnn_in['W_left'], 'L1_gnn_W_right': _L1_gnn_in['W_right'], 'L1_gnn_W_lin': _L1_gnn_in['W_lin'], 'L1_gnn_b_lin': _L1_gnn_in['b_lin'], 'L1_gnn_ln_a': _L1_gnn_in['ln_a'], 'L1_gnn_ln_b': _L1_gnn_in['ln_b']}

def reference(x, adj, L0_gnn_Wl, L0_gnn_bl, L0_gnn_Ws, L0_gnn_bs, L0_gnn_Wr, L0_gnn_br, L0_gnn_ln_w, L0_gnn_ln_b, L1_gnn_W_left, L1_gnn_W_right, L1_gnn_W_lin, L1_gnn_b_lin, L1_gnn_ln_a, L1_gnn_ln_b):
    import jax
    import jax.numpy as jnp

    def _L0_gnn_ref(hidden_state, adjacency_matrix, Wl, bl, Ws, bs, Wr, br, ln_w, ln_b):
        import jax, jax.numpy as jnp
        import numpy as np
        LN_EPS = 1e-12

        def _digcn_forward(hidden_state, adjacency_matrix, Wl, bl, Ws, bs, Wr, br, ln_w, ln_b):
            B, S, D = hidden_state.shape
            temper = jnp.asarray(D, jnp.float32) ** 0.5
            i = jnp.arange(S)
            upper = (i[None, :] > i[:, None]).astype(hidden_state.dtype)
            lower = (i[None, :] < i[:, None]).astype(hidden_state.dtype)

            def layer(h, params):
                wl, b_l, ws, b_s, wr, b_r, g, beta = params
                u = jnp.einsum('bid,bjd->bij', h, h) / temper
                a = jax.nn.softmax(u, axis=-1)
                delta = a * adjacency_matrix
                attn = delta / (jnp.sum(delta, axis=-1, keepdims=True) + 1e-10)
                hl = h @ wl.T + b_l
                hs = h @ ws.T + b_s
                hr = h @ wr.T + b_r
                diag_a = jnp.diagonal(attn, axis1=1, axis2=2)
                ctx = jnp.einsum('bij,bjd->bid', attn * upper, hl) + diag_a[..., None] * hs + jnp.einsum('bij,bjd->bid', attn * lower, hr)
                mean = ctx.mean(-1, keepdims=True)
                var = ctx.var(-1, keepdims=True)
                o = (ctx - mean) / jnp.sqrt(var + LN_EPS) * g + beta
                return (jax.nn.relu(o), None)
            out, _ = jax.lax.scan(layer, hidden_state, (Wl, bl, Ws, bs, Wr, br, ln_w, ln_b))
            return out
        return _digcn_forward(hidden_state, adjacency_matrix, Wl, bl, Ws, bs, Wr, br, ln_w, ln_b)

    def _L1_gnn_ref(hidden_state, adjacency_matrix, W_left, W_right, W_lin, b_lin, ln_a, ln_b):
        import jax, jax.numpy as jnp
        import numpy as np
        B, S, H, L = (32, 256, 384, 2)

        def _layer_norm(z, a, b, eps=0.001):
            mu = jnp.mean(z, axis=-1, keepdims=True)
            sigma = jnp.std(z, axis=-1, keepdims=True, ddof=1)
            return (z - mu) / (sigma + eps) * a + b
        temper = float(np.sqrt(H))
        adj = adjacency_matrix
        adj_tri = jnp.triu(adj, k=1)
        diag_mask = jnp.triu(adj, k=0) - adj_tri
        h = hidden_state
        for l in range(L):
            m_left = jnp.einsum('bsh,oh->bso', h, W_left[l])
            m_right = jnp.einsum('bsh,oh->bso', h, W_right[l])
            u_left = jnp.einsum('bih,bjh->bij', h, m_left) / temper
            u_right = jnp.einsum('bih,bjh->bij', h, m_right) / temper
            u = u_left * adj_tri + u_left * diag_mask + u_right * jnp.swapaxes(adj_tri, 1, 2)
            delta_exp_u = jnp.exp(u) * adj
            attention = delta_exp_u / (jnp.sum(delta_exp_u, axis=2, keepdims=True) + 1e-10)
            h_lin = jnp.einsum('bsh,oh->bso', h, W_lin[l]) + b_lin[l]
            ctx = jnp.matmul(attention, h_lin)
            h = jax.nn.relu(_layer_norm(ctx, ln_a[l], ln_b[l]))
        return h
    h = jnp.maximum(_layernorm(x, axis=-1), 0.0)
    x = x + _L0_gnn_ref(h, adj, L0_gnn_Wl, L0_gnn_bl, L0_gnn_Ws, L0_gnn_bs, L0_gnn_Wr, L0_gnn_br, L0_gnn_ln_w, L0_gnn_ln_b)
    h = jnp.maximum(_layernorm(x, axis=-1), 0.0)
    x = x + _L1_gnn_ref(h, adj, L1_gnn_W_left, L1_gnn_W_right, L1_gnn_W_lin, L1_gnn_b_lin, L1_gnn_ln_a, L1_gnn_ln_b)
    return x

_drawn_inputs = setup_inputs


def setup_inputs(seed=0):
    import zlib

    import numpy as np

    out = dict(_drawn_inputs(seed))
    spreads = {'L0_gnn_bl': (0.0, 0.1),
     'L0_gnn_bs': (0.0, 0.498),
     'L0_gnn_br': (0.0, 0.1),
     'L0_gnn_ln_w': (1.0, 0.2),
     'L0_gnn_ln_b': (0.0, 0.1),
     'L1_gnn_b_lin': (0.0, 0.1),
     'L1_gnn_ln_a': (1.0, 0.2),
     'L1_gnn_ln_b': (0.0, 0.1)}
    factors = {'L1_gnn_W_right': 8.0}
    for name, (base, spread) in spreads.items():
        noise = np.random.default_rng([zlib.crc32(name.encode()), seed]).standard_normal(out[name].shape)
        drawn = base * np.exp(spread * noise) if base else spread * noise
        out[name] = jnp.asarray(drawn.astype(out[name].dtype))
    for name, factor in factors.items():
        out[name] = (out[name] * factor).astype(out[name].dtype)
    return out
```

```python
from contextlib import ExitStack

import concourse.bass as bass
from concourse import mybir

ALU = mybir.AluOpType
ACT = mybir.ActivationFunctionType
AX_X = mybir.AxisListType.X
F32 = mybir.dt.float32
F32R = mybir.dt.float32r

P = 128
LAYERS = 4
NORM_EPS, ATT_EPS, SOFT_EPS, EXP_EPS = 1e-5, 1e-10, 1e-12, 1e-3
MIN_COLS = 256


def sections(last):
    out = []
    for l in range(LAYERS):
        out += [("E", 0, l)] + [("R", 1, 1)] * (l == 2) + [("F", 0, l)] + [("X", 1, 0)] * (l == 0)
        out += [("H", 0, l), ("T", 1, l), ("K", 0, l), ("E", 1, l)]
        out += [("R", 0, l)] * (l % 2) + [("F", 1, l)]
        ahead = l == LAYERS - 1
        out += [("X", 0, 0)] * (ahead and not last) + [("H", 1, l)]
        out += [("T", 0, (l + 1) % LAYERS)] * (not (ahead and last)) + [("K", 1, l)]
    return out + [("R", 1, 3)]


AHEAD = [("X", 0, 0), ("T", 0, 0)]
SOFT, EXPL, BOTH = (0, 1), (2, 3), (0, 1, 2, 3)


class Signal:

    def __init__(self, ctx, nc, name, keys, step=1, ahead=0):
        self.sem = ctx.enter_context(nc.semaphore(name))
        self.index = {k: n for n, k in enumerate(keys)}
        assert len(self.index) == len(keys)
        self.turn, self.step, self.ahead = len(keys), step, ahead

    def credit(self, eng):
        if self.turn > self.ahead:
            eng.sem_inc(self.sem, (self.turn - self.ahead) * self.step)

    def at(self, it, key, back=0):
        return (it + 1) * (self.turn * self.step) + (self.index[key] + 1 - back) * self.step


def program(nc, x, adj, adj_t, wl, bl, ws, bs, wr, br, ln_w, ln_b, w_left, w_right, w_lin, b_lin, ln_a, ln_b2, norm_t, out):
    G, S, D = x.shape
    NT, NC, PAIRS = S // P, D // P, G // 2
    DX = D + 2
    SCALE = float(D) ** -0.5
    LOOP, LAST = sections(False), sections(True)
    DIAG = NT

    def keys(section, layers, n, loop=LOOP):
        return [(b, l, i) for s, b, l in loop if s == section and l in layers for i in range(n)]

    def jobs_of(s, b, l):
        soft = l in SOFT
        if s == "T":
            return [("T", b, l, c) for c in range(NC)]
        if s == "E" and soft:
            return [("U", b, l, t) for t in range(NT)]
        if s == "E":
            return [("M", b, l, i) for i in range(2 * NC)]
        if s == "F" and soft:
            return [("V", b, l, i) for i in range(2 * NT)]
        if s == "F":
            return [("V", b, l, 0), ("V", b, l, 1)] + [(k, b, l, t) for t in range(NT) for k in ("UL", "UR")]
        if s == "H" and soft:
            return [("HS", b, l, t) for t in range(NT)]
        if s == "H":
            return [("V", b, l, 2), ("V", b, l, 3)]
        if s == "K":
            return [("D", b, l, i) for i in range(NT + 1) if soft] + [("C", b, l, t) for t in range(NT)]
        return []

    jobs = [j for s in LOOP for j in jobs_of(*s)]
    bank_of = {j: n % 8 for n, j in enumerate(jobs)}

    def occupants(order):
        held, before = {}, {}
        for turn in (0, 1):
            for j in [j for s in (LOOP if turn == 0 else order) for j in jobs_of(*s)]:
                before[j] = held.get(bank_of[j])
                held[bank_of[j]] = (j, turn)
        return {j: (k[0], 1 - k[1]) for j, k in before.items() if k}

    V_KEYS = [(b, l, i) for k, b, l, i in jobs if k == "V"]

    with ExitStack() as ctx:
        def sb(name, shape, dt=F32):
            return ctx.enter_context(nc.sbuf_tensor(name, shape, dt))

        def signal(name, k, step=1, ahead=0):
            return Signal(ctx, nc, name, k, step, ahead)

        bank = [ctx.enter_context(nc.psum_tensor(f"bank{i}", [P, 512], F32)) for i in range(8)]

        xs = [sb(f"x{b}", [P, NT, D]) for b in range(2)]
        adjs = [sb(f"adj{b}", [P, NT, S]) for b in range(2)]
        adjt = [sb(f"adjT{b}", [P, NT, S]) for b in range(2)]
        hthi = [sb(f"hThi{b}", [P, NC, S], F32R) for b in range(2)]
        htlo = [sb(f"hTlo{b}", [P, NC, S], F32R) for b in range(2)]
        HRING = 2
        n = sb("n", [P, NT, D])
        htf = sb("hTf", [P, HRING, S])
        e = sb("e", [P, NT, S])
        upper = sb("upper", [P, NT, P])
        lower = sb("lower", [P, NT, P])
        athi = sb("attThi", [P, NT + 1, S], F32R)
        atlo = sb("attTlo", [P, NT + 1, S], F32R)
        vhi = sb("vhi", [P, 2 * NT, D], F32R)
        vlo = sb("vlo", [P, 2 * NT, D], F32R)
        mhi = vhi[:, :, :].rearrange("p a b -> p (a b)").rearrange("p (m s) -> p m s", s=S)
        mlo = vlo[:, :, :].rearrange("p a b -> p (a b)").rearrange("p (m s) -> p m s", s=S)
        linhi = sb("linhi", [P, NT, DX], F32R)
        linlo = sb("linlo", [P, NT, DX], F32R)
        hs = sb("hs", [P, NT, D])
        RING = 2
        biased = sb("biased", [P, RING, D])
        whi = sb("whi", [P, 3, NC, D], F32R)
        wlo = sb("wlo", [P, 3, NC, D], F32R)
        wraw = sb("wraw", [P, 3, NC, D])
        bias = sb("bias", [P, 3, D])
        gb = sb("gb", [P, 2, D])
        gbt = sb("gbT", [P, 2, 2, NC])
        ident = sb("ident", [P, P])
        m_up = sb("m_up", [P, P])
        m_lo = sb("m_lo", [P, P])
        half = sb("half", [P, 2, NT])
        stats = sb("stats", [P, NT, 6])
        carrier = sb("carrier", [P, 1])
        diag_scratch = sb("diag_scratch", [P, P])
        mv = sb("mv", [P, 2, LAYERS, NT, 2])
        vecs = {k: sb(k, [P, 2, LAYERS, NT]) for k in
                ("rmax", "nmax", "esum", "dsum", "diag", "den", "rec", "rec2", "va", "vb", "root", "rs", "off")}
        xmv = sb("xmv", [P, 2, 2, NT, 2])
        xvec = {k: sb("x" + k, [P, 2, 2, NT]) for k in ("va", "root", "off")}

        x_in = [signal(f"x_in{b}", ["x"], 16, 1) for b in range(2)]
        adj_in = [signal(f"adj_in{b}", ["a"], 16, 1) for b in range(2)]
        adjt_in = [signal(f"adjT_in{b}", ["a"], 16, 1) for b in range(2)]
        w_in = [signal(f"w_in{s}", [1, 2, 3, 0], 16, 1) for s in range(3)]
        bias_in = [signal(f"bias_in{s}", [1, 2, 3, 0] if s == 2 else [1, 0], 16, 1) for s in range(3)]
        gb_in = signal("gb_in", [1, 3], 32)
        gbt_in = ctx.enter_context(nc.semaphore("gbT_in"))
        stored = [signal(f"stored{b}", ["o"], 16) for b in range(2)]
        full = {k: signal("full_" + k, [(b, l, i) for kk, b, l, i in jobs if kk == k], 1, NC * (k == "T"))
                for k in ("T", "U", "M", "V", "HS", "D", "C", "UL", "UR")}
        masks_done = ctx.enter_context(nc.semaphore("masks_done"))
        mask_step = ctx.enter_context(nc.semaphore("mask_step"))
        const_done = ctx.enter_context(nc.semaphore("const_done"))
        relu_done = signal("relu_done", keys("T", BOTH, NC), 1, NC)
        hthi_done = signal("hThi_done", keys("T", BOTH, NC), 1, NC)
        htlo_done = signal("hTlo_done", keys("T", BOTH, NC), 1, NC)
        max_done = signal("max_done", keys("E", SOFT, NT))
        nmax_done = signal("nmax_done", keys("E", SOFT, NT))
        exp_done = signal("exp_done", keys("F", BOTH, NT))
        masked_done = signal("masked_done", keys("F", SOFT, NT))
        diag_done = signal("diag_done", keys("F", SOFT, NT))
        upper_done = signal("upper_done", keys("F", SOFT, 1))
        lower_done = signal("lower_done", keys("F", SOFT, 1))
        den_done = signal("den_done", keys("F", SOFT, 1))
        rec_done = signal("rec_done", keys("F", SOFT, 1))
        rec2_done = signal("rec2_done", keys("F", SOFT, 1))
        biased_done = signal("biased_done", V_KEYS)
        vhi_done = signal("vhi_done", V_KEYS)
        vlo_done = signal("vlo_done", V_KEYS)
        hs_done = signal("hs_done", keys("H", SOFT, NT))
        dhi_done = signal("dhi_done", keys("K", SOFT, NT + 1))
        dlo_done = signal("dlo_done", keys("K", SOFT, NT + 1))
        mhi_done = signal("mhi_done", keys("E", EXPL, 2 * NC))
        mlo_done = signal("mlo_done", keys("E", EXPL, 2 * NC))
        adjr_done = signal("adjR_done", keys("F", (2,), 1))
        adjl_done = signal("adjL_done", keys("F", EXPL, 1))
        adjl2_done = signal("adjL2_done", keys("F", EXPL, 1))
        right_done = signal("right_done", keys("F", EXPL, NT))
        left_done = signal("left_done", keys("F", EXPL, NT))
        scores_done = signal("scores_done", keys("F", EXPL, NT))
        weighted_done = signal("weighted_done", keys("F", EXPL, NT))
        ahi_done = signal("ahi_done", keys("F", EXPL, NT))
        alo_done = signal("alo_done", keys("F", EXPL, NT))
        rsum_done = signal("rsum_done", keys("K", EXPL, NT))
        rrec_done = signal("rrec_done", keys("K", EXPL, NT))
        ctx_done = signal("ctx_done", keys("K", SOFT, NT))
        ectx_done = signal("ectx_done", keys("K", EXPL, NT))
        stats_done = signal("stats_done", keys("K", BOTH, NT))
        aggr_done = signal("aggr_done", keys("K", BOTH, NT))
        va_done = signal("va_done", keys("K", BOTH, 1))
        vb_done = signal("vb_done", keys("K", SOFT, 1))
        root_done = signal("root_done", keys("K", BOTH, 1))
        eps_done = signal("eps_done", keys("K", EXPL, 1))
        rs_done = signal("rs_done", keys("K", BOTH, 1))
        off_done = signal("off_done", keys("K", BOTH, 1))
        norm_done = signal("norm_done", keys("K", BOTH, NT))
        gain_done = signal("gain_done", keys("R", BOTH, NT))
        affine_done = signal("affine_done", keys("R", BOTH, NT))
        resid_done = signal("resid_done", keys("R", BOTH, NT))
        x_keys = [(b, 0 if s == "X" else 1, t) for s, b, l in LOOP if s == "X" or (s, l) == ("R", 1) for t in range(NT)]
        x_one = [(b, 0 if s == "X" else 1) for s, b, l in LOOP if s == "X" or (s, l) == ("R", 1)]
        xstats_done = signal("xstats_done", x_keys, 1, NT)
        xaggr_done = signal("xaggr_done", x_keys, 1, NT)
        xva_done = signal("xva_done", x_one, 1, 1)
        xroot_done = signal("xroot_done", x_one, 1, 1)
        xoff_done = signal("xoff_done", x_one, 1, 1)
        xnorm_done = signal("xnorm_done", x_keys, 1, NT)
        whi_done = [signal(f"whi_done{s}", [1, 2, 3, 0], 1, 1) for s in range(3)]
        wlo_done = [signal(f"wlo_done{s}", [1, 2, 3, 0], 1, 1) for s in range(3)]

        empties = {"T": relu_done, "U": exp_done, "M": mlo_done, "V": biased_done, "HS": hs_done,
                   "D": dlo_done, "UL": left_done, "UR": right_done}

        def w_turn(it, l):
            return it - (l == 0)

        def h_turn(it, b, l):
            return it - ((b, l) == (0, 0))

        def turns(eng, run, own):
            for s in own:
                s.credit(eng)
            for s in AHEAD:
                run(*s, -1, None)
            with eng.Fori(0, PAIRS - 1) as it:
                for s in LOOP:
                    run(*s, it, False)
            for s in LAST:
                run(*s, PAIRS - 1, True)

        block = ctx.enter_context(nc.Block())

        @block.sync
        def _(sp):
            w_dram = lambda s, l: ((wl, wr, ws) if l < 2 else (w_left, w_right, w_lin))[s][l % 2].rearrange("(c p) o -> p c o", p=P)
            b_dram = lambda s, l: ((bl, br, bs) if l < 2 else (None, None, b_lin))[s][l % 2:l % 2 + 1, :].partition_broadcast(P)

            def load_w(s, l, it):
                sp.dma_start(wraw[:, s], w_dram(s, l)).then_inc(w_in[s].sem, 16)

            def load_bias(s, l):
                sp.dma_start(bias[:, s, :], b_dram(s, l)).then_inc(bias_in[s].sem, 16)

            def load_x(b, pair):
                sp.dma_start(xs[b][:, :, :], x[pair * 2 + b].rearrange("(t p) d -> p t d", p=P)).then_inc(x_in[b].sem, 16)

            def load_adj(b, pair):
                sp.dma_start(adjs[b][:, :, :], adj[pair * 2 + b].rearrange("(t p) s -> p t s", p=P)).then_inc(adj_in[b].sem, 16)

            def load_adjt(b, pair):
                sp.dma_start(adjt[b][:, :, :], adj_t[pair * 2 + b].rearrange("(t p) s -> p t s", p=P)).then_inc(adjt_in[b].sem, 16)

            for s in (*w_in, *bias_in, gb_in, *stored):
                s.credit(sp)
            load_x(0, 0)
            sp.dma_start(gbt[:, :, :, :], norm_t).then_inc(gbt_in, 16)
            load_adj(0, 0)
            for s in range(3):
                load_w(s, 0, -1)
                load_bias(s, 0)
            load_x(1, 0)
            load_adj(1, 0)
            load_adjt(0, 0)
            load_adjt(1, 0)

            def run(s, b, l, it, last):
                nxt = (l + 1) % LAYERS
                if s == "E" and b == 0 and l in (0, 2):
                    prev = it - (l == 0)
                    sp.wait_ge(affine_done.sem, affine_done.at(prev, (1, 3 if l == 0 else 1, NT - 1)))
                    g_, b_ = (ln_w, ln_b) if l == 0 else (ln_a, ln_b2)
                    sp.dma_start(gb[:, 0, :], g_[1:2, :].partition_broadcast(P)).then_inc(gb_in.sem, 16)
                    sp.dma_start(gb[:, 1, :], b_[1:2, :].partition_broadcast(P)).then_inc(gb_in.sem, 16)
                if s == "F" and b == 0:
                    for w in range(3):
                        sp.wait_ge(whi_done[w].sem, whi_done[w].at(w_turn(it, l), l))
                        sp.wait_ge(wlo_done[w].sem, wlo_done[w].at(w_turn(it, l), l))
                        load_w(w, nxt, it)
                if s == "H" and b == 1:
                    if l in SOFT:
                        sp.wait_ge(hs_done.sem, hs_done.at(it, (1, l, NT - 1)))
                    else:
                        sp.wait_ge(biased_done.sem, biased_done.at(it, (1, l, NT - 1)))
                    for w in range(3):
                        if w == 2 or nxt in SOFT:
                            load_bias(w, nxt)
                if s == "H" and l == LAYERS - 1 and not last:
                    sp.wait_ge(right_done.sem, right_done.at(it, (b, l, NT - 1)))
                    load_adj(b, it + 1)
                    sp.wait_ge(left_done.sem, left_done.at(it, (b, l, NT - 1)))
                    sp.wait_ge(weighted_done.sem, weighted_done.at(it, (b, l, NT - 1)))
                    load_adjt(b, it + 1)
                if s == "R" and l == LAYERS - 1:
                    sp.wait_ge(resid_done.sem, resid_done.at(it, (b, l, NT - 1)))
                    sp.dma_start(out[it * 2 + b].rearrange("(t p) d -> p t d", p=P), xs[b][:, :, :]).then_inc(stored[b].sem, 16)
                    sp.wait_ge(stored[b].sem, stored[b].at(it, "o"))
                    if not last:
                        load_x(b, it + 1)

            with sp.Fori(0, PAIRS - 1) as it:
                for s in LOOP:
                    run(*s, it, False)
            for s in LAST:
                run(*s, PAIRS - 1, True)

        @block.tensor
        def _(pe):
            before = {False: occupants(LOOP), True: occupants(LAST)}

            def open_bank(job, it, last):
                if last is not None:
                    (k, b, l, i), turn = before[last][job]
                    s = empties[k] if k != "C" else ctx_done if l in SOFT else ectx_done
                    if not (k == "M" and job[0] in ("UL", "UR")):
                        pe.wait_ge(s.sem, s.at(it - turn, (b, l, i)))
                return bank[bank_of[job]]

            def split_product(dst, terms):
                total = 3 * len(terms)
                k = 0
                for shi, slo, rhi, rlo in terms:
                    for a, c in ((shi, rhi), (shi, rlo), (slo, rhi)):
                        ins = pe.matmul(dst, a, c, start=(k == 0), stop=(k == total - 1))
                        k += 1
                return ins

            def wait_h(b, l, it):
                pe.wait_ge(hthi_done.sem, hthi_done.at(h_turn(it, b, l), (b, l, NC - 1)))
                pe.wait_ge(htlo_done.sem, htlo_done.at(h_turn(it, b, l), (b, l, NC - 1)))

            def wait_w(s, l, it):
                pe.wait_ge(whi_done[s].sem, whi_done[s].at(w_turn(it, l), l))
                pe.wait_ge(wlo_done[s].sem, wlo_done[s].at(w_turn(it, l), l))

            def rows_times_w(job, b, t, s, it, last):
                dst = open_bank(job, it, last)
                cols = slice(t * P, (t + 1) * P)
                split_product(dst[:, 0:D], [(hthi[b][:, c, cols], htlo[b][:, c, cols], whi[:, s, c, :], wlo[:, s, c, :])
                                            for c in range(NC)]).then_inc(full[job[0]].sem, 1)

            def run(s, b, l, it, last):
                soft = l in SOFT
                for job in jobs_of(s, b, l):
                    kind, _, _, i = job
                    if kind == "T":
                        if l in (0, 2):
                            pe.wait_ge(xnorm_done.sem, xnorm_done.at(it, (b, l // 2, NT - 1)))
                        else:
                            pe.wait_ge(norm_done.sem, norm_done.at(it, (b, l - 1, NT - 1)))
                        dst = open_bank(job, it, last)
                        for t in range(NT):
                            ins = pe.transpose(dst[:, t * P:(t + 1) * P], n[:, t, i * P:(i + 1) * P], ident[:, :])
                        ins.then_inc(full["T"].sem, 1)
                    if kind == "U":
                        if i == 0:
                            wait_h(b, l, it)
                        cols = slice(i * P, (i + 1) * P)
                        dst = open_bank(job, it, last)
                        split_product(dst[:, :], [(hthi[b][:, c, cols], htlo[b][:, c, cols], hthi[b][:, c, :], htlo[b][:, c, :])
                                                  for c in range(NC)]).then_inc(full["U"].sem, 1)
                    if kind == "M":
                        side, oc = divmod(i, NC)
                        if i == 0:
                            wait_h(b, l, it)
                        if oc == 0:
                            wait_w(side, l, it)
                        cols = slice(oc * P, (oc + 1) * P)
                        dst = open_bank(job, it, last)
                        split_product(dst[:, :], [(whi[:, side, c, cols], wlo[:, side, c, cols], hthi[b][:, c, :], htlo[b][:, c, :])
                                                  for c in range(NC)]).then_inc(full["M"].sem, 1)
                    if kind == "V":
                        side, t = divmod(i, NT) if soft else (2, i)
                        if t == 0:
                            wait_w(side, l, it)
                        rows_times_w(job, b, t, side, it, last)
                    if kind == "HS":
                        if i == 0:
                            wait_w(2, l, it)
                        rows_times_w(job, b, i, 2, it, last)
                    if kind in ("UL", "UR"):
                        side = int(kind == "UR")
                        if (kind, i) == ("UL", 0):
                            pe.wait_ge(mhi_done.sem, mhi_done.at(it, (b, l, 2 * NC - 1)))
                            pe.wait_ge(mlo_done.sem, mlo_done.at(it, (b, l, 2 * NC - 1)))
                        cols = slice(i * P, (i + 1) * P)
                        to = slice(0, max((i + 1) * P, MIN_COLS)) if side == 0 else slice(min(i * P, S - MIN_COLS), S)
                        dst = open_bank(job, it, last)
                        split_product(dst[:, to], [(mhi[:, side * NC + c, cols], mlo[:, side * NC + c, cols],
                                                    hthi[b][:, c, to], htlo[b][:, c, to])
                                                   for c in range(NC)]).then_inc(full[kind].sem, 1)
                    if kind == "D":
                        if i == 0:
                            pe.wait_ge(masked_done.sem, masked_done.at(it, (b, l, NT - 1)))
                            pe.wait_ge(upper_done.sem, upper_done.at(it, (b, l, 0)))
                        if i == DIAG:
                            pe.wait_ge(lower_done.sem, lower_done.at(it, (b, l, 0)))
                        dst = open_bank(job, it, last)
                        for t in range(NT):
                            src = lower[:, t, :] if i == DIAG else upper[:, t, :] if t == i else e[:, t, i * P:(i + 1) * P]
                            ins = pe.transpose(dst[:, t * P:(t + 1) * P], src, ident[:, :])
                        ins.then_inc(full["D"].sem, 1)
                    if kind == "C" and soft:
                        if i == 0:
                            pe.wait_ge(dhi_done.sem, dhi_done.at(it, (b, l, NT)))
                            pe.wait_ge(dlo_done.sem, dlo_done.at(it, (b, l, NT)))
                            pe.wait_ge(vhi_done.sem, vhi_done.at(it, (b, l, 2 * NT - 1)))
                            pe.wait_ge(vlo_done.sem, vlo_done.at(it, (b, l, 2 * NT - 1)))
                        cols = slice(i * P, (i + 1) * P)
                        dst = open_bank(job, it, last)
                        pairs = [(j, j) for j in range(i, NT)] + [(DIAG, NT + i)] + [(j, NT + j) for j in range(i)]
                        split_product(dst[:, 0:D], [(athi[:, a, cols], atlo[:, a, cols], vhi[:, v, :], vlo[:, v, :])
                                                    for a, v in pairs]).then_inc(full["C"].sem, 1)
                    if kind == "C" and not soft:
                        if i == 0:
                            pe.wait_ge(ahi_done.sem, ahi_done.at(it, (b, l, NT - 1)))
                            pe.wait_ge(alo_done.sem, alo_done.at(it, (b, l, NT - 1)))
                            pe.wait_ge(vhi_done.sem, vhi_done.at(it, (b, l, NT - 1)))
                            pe.wait_ge(vlo_done.sem, vlo_done.at(it, (b, l, NT - 1)))
                        cols = slice(i * P, (i + 1) * P)
                        dst = open_bank(job, it, last)
                        split_product(dst[:, 0:DX], [(athi[:, j, cols], atlo[:, j, cols], linhi[:, j, :], linlo[:, j, :])
                                                     for j in range(NT)]).then_inc(full["C"].sem, 1)

            pe.wait_ge(masks_done, 3)
            pe.wait_ge(const_done, 3)
            turns(pe, run, full.values())

        def source_of(kind, b, l, i):
            return bank[bank_of[(kind, b, l, i)]]

        @block.scalar
        def _(act):
            def split_w(s, l, it):
                act.wait_ge(w_in[s].sem, w_in[s].at(it, l))
                act.activation(whi[:, s], wraw[:, s], ACT.Copy).then_inc(whi_done[s].sem, 1)

            def value_hi(b, l, i, it):
                dst = vhi[:, i, :] if l in SOFT else linhi[:, i, 0:D]
                act.wait_ge(biased_done.sem, biased_done.at(it, (b, l, i)))
                act.activation(dst, biased[:, biased_done.index[(b, l, i)] % RING, :], ACT.Copy).then_inc(vhi_done.sem, 1)

            def att_hi(b, l, t, it):
                act.wait_ge(weighted_done.sem, weighted_done.at(it, (b, l, t)))
                act.activation(athi[:, t, :], e[:, t, :], ACT.Copy).then_inc(ahi_done.sem, 1)

            def run(s, b, l, it, last):
                soft = l in SOFT
                if s == "X" or (s, l) == ("R", 1):
                    ph = 0 if s == "X" else 1
                    act.wait_ge(xoff_done.sem, xoff_done.at(it, (b, ph)))
                    if s == "X":
                        pt = (0, 0) if b == 1 else (1, 3)
                        if last is not None:
                            act.wait_ge(relu_done.sem, relu_done.at(h_turn(it, *pt), (*pt, NC - 1)))
                            act.wait_ge(resid_done.sem, resid_done.at(it - b, (b, 3, NT - 1)))
                    for t in range(NT):
                        act.activation(n[:, t, :], xs[b][:, t, :], ACT.Identity, bias=xvec["off"][:, b, ph, t:t + 1],
                                       scale=xvec["root"][:, b, ph, t:t + 1]).then_inc(xnorm_done.sem, 1)
                if s == "T":
                    for c in range(NC):
                        act.wait_ge(full["T"].sem, full["T"].at(it, (b, l, c)))
                        act.wait_ge(hthi_done.sem, hthi_done.at(it, (b, l, c), HRING))
                        act.wait_ge(htlo_done.sem, htlo_done.at(it, (b, l, c), HRING))
                        if l % 2:
                            g = l // 2
                            act.activation(htf[:, relu_done.index[(b, l, c)] % HRING, :], source_of("T", b, l, c)[:, :], ACT.Relu, bias=gbt[:, g, 1, c:c + 1],
                                           scale=gbt[:, g, 0, c:c + 1]).then_inc(relu_done.sem, 1)
                        else:
                            act.activation(htf[:, relu_done.index[(b, l, c)] % HRING, :], source_of("T", b, l, c)[:, :], ACT.Relu).then_inc(relu_done.sem, 1)
                if s == "E" and not soft:
                    for i in range(2 * NC):
                        act.wait_ge(full["M"].sem, full["M"].at(it, (b, l, i)))
                        act.activation(mhi[:, i, :], source_of("M", b, l, i)[:, :], ACT.Copy).then_inc(mhi_done.sem, 1)
                if s == "E" and soft:
                    for t in range(NT):
                        act.wait_ge(nmax_done.sem, nmax_done.at(it, (b, l, t)))
                        if t == 0:
                            act.wait_ge(diag_done.sem, diag_done.at(it, (b, l, 0), 1))
                            act.wait_ge(alo_done.sem, alo_done.at(it - 1, (1, 3, NT - 1)))
                        act.activation(e[:, t, :], source_of("U", b, l, t)[:, :], ACT.Exp, bias=vecs["nmax"][:, b, l, t:t + 1],
                                       scale=SCALE, accum_out=vecs["esum"][:, b, l, t:t + 1]).then_inc(exp_done.sem, 1)
                if s == "F" and soft:
                    for i in range(2 * NT):
                        value_hi(b, l, i, it)
                if s == "F" and not soft:
                    value_hi(b, l, 0, it)
                    value_hi(b, l, 1, it)
                    for t in range(NT):
                        act.wait_ge(scores_done.sem, scores_done.at(it, (b, l, t)))
                        act.activation(e[:, t, :], e[:, t, :], ACT.Exp, scale=SCALE).then_inc(exp_done.sem, 1)
                        if t > 0:
                            att_hi(b, l, t - 1, it)
                if s == "H" and b == 1:
                    k, i = ("V", 2 * NT - 1) if soft else ("M", 2 * NC - 1)
                    act.wait_ge(full[k].sem, full[k].at(it, (b, l, i)))
                    split_w(0, (l + 1) % LAYERS, it)
                    split_w(1, (l + 1) % LAYERS, it)
                if s == "H" and not soft:
                    att_hi(b, l, NT - 1, it)
                    value_hi(b, l, 2, it)
                    value_hi(b, l, 3, it)
                if s == "K":
                    if b == 1:
                        k, i = ("HS", NT - 1) if soft else ("V", NT - 1)
                        act.wait_ge(full[k].sem, full[k].at(it, (b, l, i)))
                        split_w(2, (l + 1) % LAYERS, it)
                    if soft:
                        for i in range(NT + 1):
                            act.wait_ge(full["D"].sem, full["D"].at(it, (b, l, i)))
                            act.activation(athi[:, i, :], source_of("D", b, l, i)[:, :], ACT.Copy).then_inc(dhi_done.sem, 1)
                    else:
                        for t in range(NT):
                            act.wait_ge(rrec_done.sem, rrec_done.at(it, (b, l, t)))
                            act.activation(n[:, t, :], source_of("C", b, l, t)[:, 0:D], ACT.Copy,
                                           scale=vecs["rec"][:, b, l, t:t + 1]).then_inc(ectx_done.sem, 1)
                    act.wait_ge(off_done.sem, off_done.at(it, (b, l, 0)))
                    for t in range(NT):
                        act.activation(n[:, t, :], n[:, t, :], ACT.Identity, bias=vecs["off"][:, b, l, t:t + 1],
                                       scale=vecs["rs"][:, b, l, t:t + 1]).then_inc(norm_done.sem, 1)

            for s in range(3):
                split_w(s, 0, -1)
            act.wait_ge(gbt_in, 16)
            turns(act, run, [relu_done, exp_done, vhi_done, dhi_done, mhi_done, ahi_done, ectx_done, norm_done, xnorm_done, *whi_done])

        @block.vector
        def _(dve):
            def add_bias(b, l, i, it):
                slot = i // NT if l in SOFT else 2
                dve.wait_ge(full["V"].sem, full["V"].at(it, (b, l, i)))
                if i % NT == 0:
                    dve.wait_ge(bias_in[slot].sem, bias_in[slot].at(w_turn(it, l), l))
                dve.wait_ge(vhi_done.sem, vhi_done.at(it, (b, l, i), RING))
                dve.wait_ge(vlo_done.sem, vlo_done.at(it, (b, l, i), RING))
                dve.tensor_tensor(biased[:, biased_done.index[(b, l, i)] % RING, :], source_of("V", b, l, i)[:, 0:D],
                                  bias[:, slot, :], ALU.add).then_inc(biased_done.sem, 1)

            def att_lo(b, l, t, it):
                dve.wait_ge(ahi_done.sem, ahi_done.at(it, (b, l, t)))
                dve.tensor_tensor(atlo[:, t, :], e[:, t, :], athi[:, t, :].bitcast(F32), ALU.subtract).then_inc(alo_done.sem, 1)

            def norm_x(b, ph, it):
                for t in range(NT):
                    dve.bn_stats(stats[:, t, :], xs[b][:, t, :]).then_inc(xstats_done.sem, 1)
                dve.wait_ge(xstats_done.sem, xstats_done.at(it, (b, ph, NT - 1)))
                dve.tensor_copy(carrier[:, :], stats[:, NT - 1, 0:1])
                for t in range(NT):
                    dve.bn_aggr(xmv[:, b, ph, t, :], stats[:, t, :]).then_inc(xaggr_done.sem, 1)
                dve.wait_ge(xaggr_done.sem, xaggr_done.at(it, (b, ph, NT - 1)))
                dve.tensor_scalar(xvec["va"][:, b, ph, :], xmv[:, b, ph, :, 1], NORM_EPS, None, ALU.add).then_inc(xva_done.sem, 1)
                dve.wait_ge(xroot_done.sem, xroot_done.at(it, (b, ph)))
                dve.scalar_tensor_tensor(out=xvec["off"][:, b, ph, :], in0=xmv[:, b, ph, :, 0], scalar=-1.0,
                                         in1=xvec["root"][:, b, ph, :], op0=ALU.mult, op1=ALU.mult).then_inc(xoff_done.sem, 1)

            def run(s, b, l, it, last):
                soft = l in SOFT
                v = {k: t[:, b, l, :] for k, t in vecs.items()}
                if s == "X":
                    dve.wait_ge(x_in[b].sem, x_in[b].at(it - b, "x"))
                    norm_x(b, 0, it)
                if s == "T":
                    for c in range(NC):
                        dve.wait_ge(relu_done.sem, relu_done.at(it, (b, l, c)))
                        dve.tensor_copy(hthi[b][:, c, :], htf[:, relu_done.index[(b, l, c)] % HRING, :]).then_inc(hthi_done.sem, 1)
                if s == "E" and soft:
                    for t in range(NT):
                        dve.wait_ge(full["U"].sem, full["U"].at(it, (b, l, t)))
                        dve.tensor_reduce(v["rmax"][:, t:t + 1], source_of("U", b, l, t)[:, :], AX_X, ALU.max).then_inc(max_done.sem, 1)
                        dve.wait_ge(max_done.sem, max_done.at(it, (b, l, t)))
                        dve.tensor_scalar(v["nmax"][:, t:t + 1], v["rmax"][:, t:t + 1], -SCALE, None, ALU.mult).then_inc(nmax_done.sem, 1)
                if s == "E" and not soft:
                    for i in range(2 * NC):
                        dve.wait_ge(mhi_done.sem, mhi_done.at(it, (b, l, i)))
                        dve.tensor_tensor(mlo[:, i, :], source_of("M", b, l, i)[:, :], mhi[:, i, :].bitcast(F32),
                                          ALU.subtract).then_inc(mlo_done.sem, 1)
                if s == "F" and soft:
                    if l == 0:
                        dve.wait_ge(adj_in[b].sem, adj_in[b].at(it - 1, "a"))
                    for i in range(2 * NT):
                        add_bias(b, l, i, it)
                        if i < NT:
                            dve.wait_ge(exp_done.sem, exp_done.at(it, (b, l, i)))
                            dve.tensor_tensor_reduce(e[:, i, :], e[:, i, :], adjs[b][:, i, :], 1.0, 0.0, ALU.mult, ALU.add,
                                                     v["dsum"][:, i:i + 1]).then_inc(masked_done.sem, 1)
                        else:
                            t = i - NT
                            dve.wait_ge(masked_done.sem, masked_done.at(it, (b, l, t)))
                            dve.wait_ge(diag_done.sem, diag_done.at(it, (b, l, t), 1))
                            dve.tensor_tensor_reduce(diag_scratch[:, :], e[:, t, t * P:(t + 1) * P], ident[:, :], 1.0, 0.0,
                                                     ALU.mult, ALU.add, v["diag"][:, t:t + 1]).then_inc(diag_done.sem, 1)
                    dve.scalar_tensor_tensor(out=v["den"], in0=v["esum"], scalar=ATT_EPS, in1=v["dsum"],
                                             op0=ALU.mult, op1=ALU.add).then_inc(den_done.sem, 1)
                    dve.wait_ge(den_done.sem, den_done.at(it, (b, l, 0)))
                    dve.reciprocal(v["rec"], v["den"]).then_inc(rec_done.sem, 1)
                    dve.wait_ge(rec_done.sem, rec_done.at(it, (b, l, 0)))
                    dve.tensor_tensor(v["rec2"], v["rec"], v["rec"], ALU.mult).then_inc(rec2_done.sem, 1)
                if s == "F" and not soft:
                    add_bias(b, l, 0, it)
                    add_bias(b, l, 1, it)
                    if l == 2:
                        dve.wait_ge(adjr_done.sem, adjr_done.at(it, (b, l, 0)))
                    dve.wait_ge(adjl2_done.sem, adjl2_done.at(it, (b, l, 0)))
                    for t in range(NT):
                        lo = t * P
                        dve.wait_ge(full["UL"].sem, full["UL"].at(it, (b, l, t)))
                        if t == 0:
                            dve.wait_ge(ahi_done.sem, ahi_done.at(it, (b, l, 0), 1))
                        if t > 0:
                            dve.tensor_tensor(e[:, t, 0:lo], source_of("UL", b, l, t)[:, 0:lo], adjt[b][:, t, 0:lo], ALU.mult)
                        dve.tensor_tensor(lower[:, t, :], source_of("UL", b, l, t)[:, lo:lo + P], upper[:, t, :],
                                          ALU.mult).then_inc(left_done.sem, 1)
                        dve.wait_ge(full["UR"].sem, full["UR"].at(it, (b, l, t)))
                        dve.tensor_tensor(e[:, t, lo:S], source_of("UR", b, l, t)[:, lo:S], adjs[b][:, t, lo:S],
                                          ALU.mult).then_inc(right_done.sem, 1)
                        if t >= 2:
                            att_lo(b, l, t - 2, it)
                if s == "H" and soft:
                    dve.wait_ge(bias_in[2].sem, bias_in[2].at(w_turn(it, l), l))
                    for t in range(NT):
                        dve.wait_ge(full["HS"].sem, full["HS"].at(it, (b, l, t)))
                        dve.tensor_tensor(hs[:, t, :], source_of("HS", b, l, t)[:, 0:D], bias[:, 2, :], ALU.add).then_inc(hs_done.sem, 1)
                if s == "H" and not soft:
                    att_lo(b, l, NT - 2, it)
                    add_bias(b, l, 2, it)
                    att_lo(b, l, NT - 1, it)
                    add_bias(b, l, 3, it)
                if s == "K":
                    if soft:
                        for i in range(NT + 1):
                            dve.wait_ge(dhi_done.sem, dhi_done.at(it, (b, l, i)))
                            dve.tensor_tensor(atlo[:, i, :], source_of("D", b, l, i)[:, :], athi[:, i, :].bitcast(F32),
                                              ALU.subtract).then_inc(dlo_done.sem, 1)
                        dve.wait_ge(hs_done.sem, hs_done.at(it, (b, l, NT - 1)))
                        dve.wait_ge(diag_done.sem, diag_done.at(it, (b, l, NT - 1)))
                    for t in range(NT):
                        dve.wait_ge(full["C"].sem, full["C"].at(it, (b, l, t)))
                        if soft:
                            dve.scalar_tensor_tensor(out=n[:, t, :], in0=hs[:, t, :], scalar=v["diag"][:, t:t + 1],
                                                     in1=source_of("C", b, l, t)[:, 0:D], op0=ALU.mult, op1=ALU.add).then_inc(ctx_done.sem, 1)
                            dve.wait_ge(ctx_done.sem, ctx_done.at(it, (b, l, t)))
                        else:
                            dve.tensor_scalar(v["den"][:, t:t + 1], source_of("C", b, l, t)[:, D:D + 1], ATT_EPS, None,
                                              ALU.add).then_inc(rsum_done.sem, 1)
                            dve.wait_ge(rsum_done.sem, rsum_done.at(it, (b, l, t)))
                            dve.reciprocal(v["rec"][:, t:t + 1], v["den"][:, t:t + 1]).then_inc(rrec_done.sem, 1)
                            dve.wait_ge(ectx_done.sem, ectx_done.at(it, (b, l, t)))
                        dve.bn_stats(stats[:, t, :], n[:, t, :]).then_inc(stats_done.sem, 1)
                    dve.wait_ge(stats_done.sem, stats_done.at(it, (b, l, NT - 1)))
                    dve.tensor_copy(carrier[:, :], stats[:, NT - 1, 0:1])
                    for t in range(NT):
                        dve.bn_aggr(mv[:, b, l, t, :], stats[:, t, :]).then_inc(aggr_done.sem, 1)
                    dve.wait_ge(aggr_done.sem, aggr_done.at(it, (b, l, NT - 1)))
                    mean, var = mv[:, b, l, :, 0], mv[:, b, l, :, 1]
                    if soft:
                        dve.tensor_tensor(v["va"], var, v["rec2"], ALU.mult).then_inc(va_done.sem, 1)
                        dve.wait_ge(va_done.sem, va_done.at(it, (b, l, 0)))
                        dve.tensor_scalar(v["vb"], v["va"], SOFT_EPS, None, ALU.add).then_inc(vb_done.sem, 1)
                        dve.wait_ge(root_done.sem, root_done.at(it, (b, l, 0)))
                        dve.tensor_tensor(v["rs"], v["root"], v["rec"], ALU.mult).then_inc(rs_done.sem, 1)
                    else:
                        dve.tensor_scalar(v["va"], var, float(D) / (D - 1), None, ALU.mult).then_inc(va_done.sem, 1)
                        dve.wait_ge(root_done.sem, root_done.at(it, (b, l, 0)))
                        dve.tensor_scalar(v["vb"], v["root"], EXP_EPS, None, ALU.add).then_inc(eps_done.sem, 1)
                        dve.wait_ge(eps_done.sem, eps_done.at(it, (b, l, 0)))
                        dve.reciprocal(v["rs"], v["vb"]).then_inc(rs_done.sem, 1)
                    dve.wait_ge(rs_done.sem, rs_done.at(it, (b, l, 0)))
                    dve.scalar_tensor_tensor(out=v["off"], in0=mean, scalar=-1.0, in1=v["rs"],
                                             op0=ALU.mult, op1=ALU.mult).then_inc(off_done.sem, 1)
                if s == "R":
                    for t in range(NT):
                        dve.wait_ge(affine_done.sem, affine_done.at(it, (b, l, t)))
                        dve.scalar_tensor_tensor(out=xs[b][:, t, :], in0=n[:, t, :], scalar=0.0, in1=xs[b][:, t, :],
                                                 op0=ALU.max, op1=ALU.add).then_inc(resid_done.sem, 1)
                    if l == 1:
                        dve.wait_ge(resid_done.sem, resid_done.at(it, (b, l, NT - 1)))
                        norm_x(b, 1, it)

            dve.memset(half[:, 0, :], 0.5).then_inc(const_done, 1)
            dve.memset(half[:, 1, :], -0.5).then_inc(const_done, 1)
            dve.memset(linhi[:, :, D:DX].bitcast(F32), 1.0).then_inc(const_done, 1)
            dve.memset(linlo[:, :, D:DX].bitcast(F32), 0.0).then_inc(const_done, 1)
            dve.wait_ge(masks_done, 3)
            turns(dve, run, [hthi_done, max_done, nmax_done, masked_done, diag_done, den_done, rec_done, rec2_done, biased_done,
                             hs_done, dlo_done, mlo_done, right_done, left_done, alo_done, rsum_done, rrec_done, ctx_done,
                             stats_done, aggr_done, va_done, vb_done, eps_done, rs_done, off_done, resid_done,
                             xstats_done, xaggr_done, xva_done, xoff_done])

        @block.gpsimd
        def _(pool):
            def split_w(s, l, it):
                pool.wait_ge(whi_done[s].sem, whi_done[s].at(it, l))
                pool.tensor_tensor(wlo[:, s], wraw[:, s], whi[:, s].bitcast(F32), ALU.subtract).then_inc(wlo_done[s].sem, 1)

            def value_lo(b, l, i, it):
                hi, dst = (vhi[:, i, :], vlo[:, i, :]) if l in SOFT else (linhi[:, i, 0:D], linlo[:, i, 0:D])
                pool.wait_ge(vhi_done.sem, vhi_done.at(it, (b, l, i)))
                pool.tensor_tensor(dst, biased[:, biased_done.index[(b, l, i)] % RING, :], hi.bitcast(F32),
                                   ALU.subtract).then_inc(vlo_done.sem, 1)

            def diagonal(a):
                v = a[:, :, :].rearrange("p t s -> p (t s)")
                return [v[:, t * (S + P):t * (S + P) + P] for t in range(NT)]

            def weigh(b, l, t, it):
                pool.wait_ge(exp_done.sem, exp_done.at(it, (b, l, t)))
                pool.tensor_tensor(e[:, t, :], e[:, t, :], adjt[b][:, t, :], ALU.mult).then_inc(weighted_done.sem, 1)

            def run(s, b, l, it, last):
                soft = l in SOFT
                if s == "T":
                    for c in range(NC):
                        pool.wait_ge(hthi_done.sem, hthi_done.at(it, (b, l, c)))
                        pool.tensor_tensor(htlo[b][:, c, :], htf[:, relu_done.index[(b, l, c)] % HRING, :], hthi[b][:, c, :].bitcast(F32),
                                           ALU.subtract).then_inc(htlo_done.sem, 1)
                if s == "F" and soft:
                    for i in range(NT):
                        value_lo(b, l, i, it)
                    pool.wait_ge(masked_done.sem, masked_done.at(it, (b, l, NT - 1)))
                    for mask, dst, done in ((m_up, upper, upper_done), (m_lo, lower, lower_done)):
                        for t, blk in enumerate(diagonal(e)):
                            ins = pool.tensor_tensor(dst[:, t, :], blk, mask[:, :], ALU.mult)
                        ins.then_inc(done.sem, 1)
                    for i in range(NT, 2 * NT):
                        value_lo(b, l, i, it)
                if s == "F" and not soft:
                    if l == 2:
                        pool.wait_ge(masked_done.sem, masked_done.at(it, (b, 1, NT - 1)))
                        for blk in diagonal(adjs[b]):
                            ins = pool.tensor_tensor(blk, blk, m_up[:, :], ALU.mult)
                        ins.then_inc(adjr_done.sem, 1)
                        pool.wait_ge(adjt_in[b].sem, adjt_in[b].at(it - 1, "a"))
                    pool.wait_ge(left_done.sem, left_done.at(it, (b, l, 0), 1))
                    if l == 2 and b == 0:
                        pool.wait_ge(full["D"].sem, full["D"].at(it, (1, 1, NT)))
                    for t, blk in enumerate(diagonal(adjt[b])):
                        ins = pool.tensor_tensor(upper[:, t, :], blk, m_up[:, :], ALU.mult)
                    ins.then_inc(adjl_done.sem, 1)
                    pool.wait_ge(adjl_done.sem, adjl_done.at(it, (b, l, 0)))
                    for t, blk in enumerate(diagonal(adjt[b])):
                        ins = pool.tensor_tensor(upper[:, t, :], blk, upper[:, t, :], ALU.subtract)
                    ins.then_inc(adjl2_done.sem, 1)
                    value_lo(b, l, 0, it)
                    value_lo(b, l, 1, it)
                    for t in range(NT):
                        blk = diagonal(e)[t]
                        pool.wait_ge(right_done.sem, right_done.at(it, (b, l, t)))
                        pool.tensor_tensor(blk, blk, lower[:, t, :], ALU.add).then_inc(scores_done.sem, 1)
                        if t > 0:
                            weigh(b, l, t - 1, it)
                if s == "H" and b == 1:
                    split_w(0, (l + 1) % LAYERS, it)
                    split_w(1, (l + 1) % LAYERS, it)
                if s == "H" and not soft:
                    weigh(b, l, NT - 1, it)
                    value_lo(b, l, 2, it)
                    value_lo(b, l, 3, it)
                if s == "K":
                    if b == 1:
                        split_w(2, (l + 1) % LAYERS, it)
                    src = vb_done if soft else va_done
                    pool.wait_ge(src.sem, src.at(it, (b, l, 0)))
                    pool.tensor_tensor(vecs["root"][:, b, l, :], vecs["vb" if soft else "va"][:, b, l, :],
                                       half[:, 1 if soft else 0, :], ALU.pow).then_inc(root_done.sem, 1)
                if s == "R":
                    pool.wait_ge(gb_in.sem, gb_in.at(it, l))
                    for t in range(NT):
                        pool.wait_ge(norm_done.sem, norm_done.at(it, (b, l, t)))
                        pool.tensor_tensor(n[:, t, :], n[:, t, :], gb[:, 0, :], ALU.mult).then_inc(gain_done.sem, 1)
                        pool.wait_ge(gain_done.sem, gain_done.at(it, (b, l, t)))
                        pool.tensor_tensor(n[:, t, :], n[:, t, :], gb[:, 1, :], ALU.add).then_inc(affine_done.sem, 1)
                if s == "X" or (s, l) == ("R", 1):
                    ph = 0 if s == "X" else 1
                    pool.wait_ge(xva_done.sem, xva_done.at(it, (b, ph)))
                    pool.tensor_tensor(xvec["root"][:, b, ph, :], xvec["va"][:, b, ph, :], half[:, 1, :],
                                       ALU.pow).then_inc(xroot_done.sem, 1)

            for m in (ident, m_up, m_lo):
                pool.memset(m[:, :], 1.0).then_inc(mask_step, 1)
            pool.wait_ge(mask_step, 3)
            for m, op, sign in ((ident, ALU.is_equal, 1), (m_up, ALU.is_gt, 1), (m_lo, ALU.is_gt, -1)):
                pool.affine_select(out=m[:, :], in_=m[:, :], compare_op=op, fill=0.0, base=0,
                                   pattern=[[sign, P]], channel_multiplier=-sign).then_inc(masks_done, 1)
            pool.wait_ge(masks_done, 3)
            pool.wait_ge(const_done, 4)
            for s in range(3):
                split_w(s, 0, -1)
            turns(pool, run, [htlo_done, upper_done, lower_done, vlo_done, adjr_done, adjl_done, adjl2_done, scores_done,
                              weighted_done, root_done, gain_done, affine_done, xroot_done, *wlo_done])


_NAMES = ["L0_gnn_Wl", "L0_gnn_bl", "L0_gnn_Ws", "L0_gnn_bs", "L0_gnn_Wr", "L0_gnn_br", "L0_gnn_ln_w", "L0_gnn_ln_b",
          "L1_gnn_W_left", "L1_gnn_W_right", "L1_gnn_W_lin", "L1_gnn_b_lin", "L1_gnn_ln_a", "L1_gnn_ln_b"]


def kernel(**inputs):
    import numpy as _np
    import concourse.bacc as _bacc
    from concourse import mybir as _mybir
    from concourse.bass_utils import run_bass_kernel_spmd as _run

    nc = _bacc.Bacc("TRN2", target_bir_lowering=False, num_devices=1)
    arrays, args = {}, []

    def give(name, a):
        a = _np.ascontiguousarray(a)
        arrays[f"in_{name}_dram"] = a
        args.append(nc.dram_tensor(f"in_{name}_dram", a.shape, _mybir.dt.from_np(a.dtype), kind="ExternalInput").ap())

    x = _np.asarray(inputs["x"])
    adj = _np.asarray(inputs["adj"])
    give("x", x)
    give("adj", adj)
    give("adj_t", adj.transpose(0, 2, 1))
    for name in _NAMES:
        a = _np.asarray(inputs[name])
        give(name, a.transpose(0, 2, 1) if a.ndim == 3 else a)
    norms = _np.stack([_np.asarray(inputs[k])[0] for k in ("L0_gnn_ln_w", "L0_gnn_ln_b", "L1_gnn_ln_a", "L1_gnn_ln_b")])
    give("norm_t", norms.reshape(2, 2, -1, P).transpose(3, 0, 1, 2))
    out = nc.dram_tensor("out_0_dram", x.shape, _mybir.dt.float32, kind="ExternalOutput").ap()
    program(nc, *args, out)
    r = _run(nc, [arrays], core_ids=[0])
    return r.results[0]["out_0_dram"]
```

```python
from contextlib import ExitStack

import concourse.bass as bass
from concourse import mybir

ALU = mybir.AluOpType
ACT = mybir.ActivationFunctionType
AX_X = mybir.AxisListType.X
F32 = mybir.dt.float32
F32R = mybir.dt.float32r

P = 128
LAYERS = 4
NORM_EPS, ATT_EPS, SOFT_EPS, EXP_EPS = 1e-5, 1e-10, 1e-12, 1e-3
MIN_COLS = 256


def sections(last):
    out = []
    for l in range(LAYERS):
        ahead = l == LAYERS - 1
        out += [("E", 0, l)] + [("N", 1, 1), ("Z", 1, 1)] * (l == 2) + [("F", 0, l)] + [("X", 1, 0)] * (l == 0)
        out += [("H", 0, l)] + [("Z", 1, 0)] * (l == 0) + [("D", 0, l), ("T", 1, l), ("K", 0, l)] + [("R", 0, l)] * (l % 2)
        out += [("E", 1, l)] + [("X", 0, 0), ("Z", 0, 0)] * (ahead and not last)
        out += [("F", 1, l)] + [("N", 0, 1)] * (l == 1) + [("H", 1, l)] + [("Z", 0, 1)] * (l == 1) + [("D", 1, l)]
        out += [("T", 0, (l + 1) % LAYERS)] * (not (ahead and last)) + [("K", 1, l)] + [("R", 1, l)] * (l % 2)
    return out


AHEAD = [("X", 0, 0), ("Z", 0, 0), ("T", 0, 0)]
SOFT, EXPL, BOTH = (0, 1), (2, 3), (0, 1, 2, 3)


class Signal:

    def __init__(self, ctx, nc, name, keys, step=1, ahead=0):
        self.sem = ctx.enter_context(nc.semaphore(name))
        self.index = {k: n for n, k in enumerate(keys)}
        assert len(self.index) == len(keys)
        self.turn, self.step, self.ahead = len(keys), step, ahead

    def credit(self, eng):
        if self.turn > self.ahead:
            eng.sem_inc(self.sem, (self.turn - self.ahead) * self.step)

    def at(self, it, key, back=0):
        return (it + 1) * (self.turn * self.step) + (self.index[key] + 1 - back) * self.step


def program(nc, x, adj, adj_t, wl, bl, ws, bs, wr, br, ln_w, ln_b, w_left, w_right, w_lin, b_lin, ln_a, ln_b2, norm_t, out):
    G, S, D = x.shape
    NT, NC, PAIRS = S // P, D // P, G // 2
    DX = D + 2
    SCALE = float(D) ** -0.5
    LOOP, LAST = sections(False), sections(True)
    DIAG = NT

    def keys(section, layers, n, loop=LOOP):
        return [(b, l, i) for s, b, l in loop if s == section and l in layers for i in range(n)]

    def jobs_of(s, b, l):
        soft = l in SOFT
        if s == "T":
            return [("T", b, l, c) for c in range(NC)]
        if s == "E" and soft:
            return [("U", b, l, t) for t in range(NT)]
        if s == "E":
            return [("M", b, l, i) for i in range(2 * NC)]
        if s == "F" and soft:
            return [("V", b, l, i) for i in range(2 * NT)]
        if s == "F":
            return [("V", b, l, 0)] + [(k, b, l, t) for t in range(NT) for k in ("UL", "UR")]
        if s == "H" and soft:
            return [("HS", b, l, t) for t in range(NT)]
        if s == "H":
            return [("V", b, l, t) for t in range(1, NT)]
        if s == "D":
            return [("D", b, l, i) for i in range(NT + 1) if soft]
        if s == "K":
            return [("C", b, l, t) for t in range(NT)]
        return []

    jobs = [j for s in LOOP for j in jobs_of(*s)]
    bank_of = {j: n % 8 for n, j in enumerate(jobs)}

    def occupants(order):
        held, before = {}, {}
        for turn in (0, 1):
            for j in [j for s in (LOOP if turn == 0 else order) for j in jobs_of(*s)]:
                before[j] = held.get(bank_of[j])
                held[bank_of[j]] = (j, turn)
        return {j: (k[0], 1 - k[1]) for j, k in before.items() if k}

    V_KEYS = [(b, l, i) for k, b, l, i in jobs if k == "V"]

    with ExitStack() as ctx:
        def sb(name, shape, dt=F32):
            return ctx.enter_context(nc.sbuf_tensor(name, shape, dt))

        def signal(name, k, step=1, ahead=0):
            return Signal(ctx, nc, name, k, step, ahead)

        bank = [ctx.enter_context(nc.psum_tensor(f"bank{i}", [P, 512], F32)) for i in range(8)]

        xs = [sb(f"x{b}", [P, NT, D]) for b in range(2)]
        adjs = [sb(f"adj{b}", [P, NT, S]) for b in range(2)]
        adjt = [sb(f"adjT{b}", [P, NT, S]) for b in range(2)]
        hthi = [sb(f"hThi{b}", [P, NC, S], F32R) for b in range(2)]
        htlo = [sb(f"hTlo{b}", [P, NC, S], F32R) for b in range(2)]
        HRING = 2
        n = sb("n", [P, NT, D])
        htf = sb("hTf", [P, HRING, S])
        e = sb("e", [P, NT, S])
        upper = sb("upper", [P, NT, P])
        lower = sb("lower", [P, NT, P])
        athi = sb("attThi", [P, NT + 1, S], F32R)
        atlo = sb("attTlo", [P, NT + 1, S], F32R)
        vhi = sb("vhi", [P, 2 * NT, D], F32R)
        vlo = sb("vlo", [P, 2 * NT, D], F32R)
        mhi = vhi[:, :, :].rearrange("p a b -> p (a b)").rearrange("p (m s) -> p m s", s=S)
        mlo = vlo[:, :, :].rearrange("p a b -> p (a b)").rearrange("p (m s) -> p m s", s=S)
        linhi = sb("linhi", [P, NT, DX], F32R)
        linlo = sb("linlo", [P, NT, DX], F32R)
        hs = sb("hs", [P, NT, D])
        RING = 2
        biased = sb("biased", [P, RING, D])
        whi = sb("whi", [P, 3, NC, D], F32R)
        wlo = sb("wlo", [P, 3, NC, D], F32R)
        wraw = sb("wraw", [P, 3, NC, D])
        bias = sb("bias", [P, 3, D])
        gb = sb("gb", [P, 2, D])
        gbt = sb("gbT", [P, 2, 2, NC])
        ident = sb("ident", [P, P])
        m_up = sb("m_up", [P, P])
        m_lo = sb("m_lo", [P, P])
        half = sb("half", [P, 2, NT])
        stats = sb("stats", [P, NT, 6])
        carrier = sb("carrier", [P, 1])
        diag_scratch = sb("diag_scratch", [P, P])
        mv = sb("mv", [P, 2, LAYERS, NT, 2])
        vecs = {k: sb(k, [P, 2, LAYERS, NT]) for k in
                ("rmax", "nmax", "esum", "dsum", "diag", "den", "rec", "rec2", "va", "vb", "root", "rs", "off")}
        xmv = sb("xmv", [P, 2, 2, NT, 2])
        xvec = {k: sb("x" + k, [P, 2, 2, NT]) for k in ("va", "root", "off")}

        x_in = [signal(f"x_in{b}", ["x"], 16, 1) for b in range(2)]
        adj_in = [signal(f"adj_in{b}", ["a"], 16, 1) for b in range(2)]
        adjt_in = [signal(f"adjT_in{b}", ["a"], 16, 1) for b in range(2)]
        w_in = [signal(f"w_in{s}", [1, 2, 3, 0], 16, 1) for s in range(3)]
        bias_in = [signal(f"bias_in{s}", [1, 2, 3, 0] if s == 2 else [1, 0], 16, 1) for s in range(3)]
        gb_in = signal("gb_in", [1, 3], 32)
        gbt_in = ctx.enter_context(nc.semaphore("gbT_in"))
        stored = [signal(f"stored{b}", ["o"], 32) for b in range(2)]
        full = {k: signal("full_" + k, [(b, l, i) for kk, b, l, i in jobs if kk == k], 1, NC * (k == "T"))
                for k in ("T", "U", "M", "V", "HS", "D", "C", "UL", "UR")}
        masks_done = ctx.enter_context(nc.semaphore("masks_done"))
        mask_step = ctx.enter_context(nc.semaphore("mask_step"))
        const_done = ctx.enter_context(nc.semaphore("const_done"))
        relu_done = signal("relu_done", keys("T", BOTH, NC), 1, NC)
        hthi_done = signal("hThi_done", keys("T", BOTH, NC), 1, NC)
        htlo_done = signal("hTlo_done", keys("T", BOTH, NC), 1, NC)
        max_done = signal("max_done", keys("E", SOFT, NT))
        nmax_done = signal("nmax_done", keys("E", SOFT, NT))
        exp_done = signal("exp_done", keys("F", BOTH, NT))
        masked_done = signal("masked_done", keys("F", SOFT, NT))
        diag_done = signal("diag_done", keys("F", SOFT, NT))
        upper_done = signal("upper_done", keys("F", SOFT, NT))
        lower_done = signal("lower_done", keys("F", SOFT, NT))
        den_done = signal("den_done", keys("F", SOFT, 1))
        rec_done = signal("rec_done", keys("F", SOFT, 1))
        rec2_done = signal("rec2_done", keys("F", SOFT, 1))
        biased_done = signal("biased_done", V_KEYS)
        vhi_done = signal("vhi_done", V_KEYS)
        vlo_done = signal("vlo_done", V_KEYS)
        hs_done = signal("hs_done", keys("H", SOFT, NT))
        dhi_done = signal("dhi_done", keys("D", SOFT, NT + 1))
        dlo_done = signal("dlo_done", keys("D", SOFT, NT + 1))
        mhi_done = signal("mhi_done", keys("E", EXPL, 2 * NC))
        mlo_done = signal("mlo_done", keys("E", EXPL, 2 * NC))
        adjr_done = signal("adjR_done", keys("E", (2,), 1))
        adjl_done = signal("adjL_done", keys("E", EXPL, 1))
        adjl2_done = signal("adjL2_done", keys("E", EXPL, 1))
        right_done = signal("right_done", keys("F", EXPL, NT))
        left_done = signal("left_done", keys("F", EXPL, NT))
        scores_done = signal("scores_done", keys("F", EXPL, NT))
        weighted_done = signal("weighted_done", keys("F", EXPL, NT))
        ahi_done = signal("ahi_done", keys("F", EXPL, NT))
        alo_done = signal("alo_done", keys("F", EXPL, NT))
        rsum_done = signal("rsum_done", keys("K", EXPL, NT))
        rrec_done = signal("rrec_done", keys("K", EXPL, NT))
        ctx_done = signal("ctx_done", keys("K", SOFT, NT))
        ectx_done = signal("ectx_done", keys("K", EXPL, NT))
        stats_done = signal("stats_done", keys("K", BOTH, NT))
        aggr_done = signal("aggr_done", keys("K", BOTH, NT))
        va_done = signal("va_done", keys("K", BOTH, 1))
        vb_done = signal("vb_done", keys("K", SOFT, 1))
        root_done = signal("root_done", keys("K", BOTH, 1))
        eps_done = signal("eps_done", keys("K", EXPL, 1))
        rs_done = signal("rs_done", keys("K", BOTH, 1))
        off_done = signal("off_done", keys("K", BOTH, 1))
        norm_done = signal("norm_done", keys("K", BOTH, NT))
        gain_done = signal("gain_done", keys("R", BOTH, NT))
        affine_done = signal("affine_done", keys("R", BOTH, NT))
        resid_done = signal("resid_done", keys("R", BOTH, NT))
        x_keys = [(b, 0 if s == "X" else 1, t) for s, b, l in LOOP if s in "XN" for t in range(NT)]
        x_one = [(b, 0 if s == "X" else 1) for s, b, l in LOOP if s in "XN"]
        z_one = [(b, ph) for s, b, ph in LOOP if s == "Z"]
        xstats_done = signal("xstats_done", x_keys, 1, NT)
        xaggr_done = signal("xaggr_done", x_keys, 1, NT)
        xva_done = signal("xva_done", x_one, 1, 1)
        xroot_done = signal("xroot_done", x_one, 1, 1)
        xoff_done = signal("xoff_done", z_one, 1, 1)
        xnorm_done = signal("xnorm_done", [(b, ph, t) for b, ph in z_one for t in range(NT)], 1, NT)
        whi_done = [signal(f"whi_done{s}", [1, 2, 3, 0], 1, 1) for s in range(3)]
        wlo_done = [signal(f"wlo_done{s}", [1, 2, 3, 0], 1, 1) for s in range(3)]

        empties = {"T": relu_done, "U": exp_done, "M": mlo_done, "V": biased_done, "HS": hs_done,
                   "D": dlo_done, "UL": left_done, "UR": right_done}

        def w_turn(it, l):
            return it - (l == 0)

        def h_turn(it, b, l):
            return it - ((b, l) == (0, 0))

        def turns(eng, run, own, split_w=None):
            for s in own:
                s.credit(eng)
            for s in AHEAD:
                run(*s, -1, None)
            if split_w:
                for s in range(3):
                    split_w(s, 0, -1)
            with eng.Fori(0, PAIRS - 1) as it:
                for s in LOOP:
                    run(*s, it, False)
            for s in LAST:
                run(*s, PAIRS - 1, True)

        block = ctx.enter_context(nc.Block())

        @block.sync
        def _(sp):
            w_dram = lambda s, l: ((wl, wr, ws) if l < 2 else (w_left, w_right, w_lin))[s][l % 2].rearrange("(c p) o -> p c o", p=P)
            b_dram = lambda s, l: ((bl, br, bs) if l < 2 else (None, None, b_lin))[s][l % 2:l % 2 + 1, :].partition_broadcast(P)

            def load_w(s, l, it):
                sp.dma_start(wraw[:, s], w_dram(s, l)).then_inc(w_in[s].sem, 16)

            def load_bias(s, l):
                sp.dma_start(bias[:, s, :], b_dram(s, l)).then_inc(bias_in[s].sem, 16)

            def load_x(b, pair):
                sp.dma_start(xs[b][:, :, :], x[pair * 2 + b].rearrange("(t p) d -> p t d", p=P)).then_inc(x_in[b].sem, 16)

            def load_adj(b, pair):
                sp.dma_start(adjs[b][:, :, :], adj[pair * 2 + b].rearrange("(t p) s -> p t s", p=P)).then_inc(adj_in[b].sem, 16)

            def load_adjt(b, pair):
                sp.dma_start(adjt[b][:, :, :], adj_t[pair * 2 + b].rearrange("(t p) s -> p t s", p=P)).then_inc(adjt_in[b].sem, 16)

            for s in (*w_in, *bias_in, gb_in, *stored):
                s.credit(sp)
            load_x(0, 0)
            sp.dma_start(gbt[:, :, :, :], norm_t).then_inc(gbt_in, 16)
            load_adj(0, 0)
            for s in range(3):
                load_w(s, 0, -1)
                load_bias(s, 0)
            load_x(1, 0)
            load_adj(1, 0)
            load_adjt(0, 0)
            load_adjt(1, 0)

            def run(s, b, l, it, last):
                nxt = (l + 1) % LAYERS
                if s == "E" and b == 0 and l in (0, 2):
                    prev = it - (l == 0)
                    sp.wait_ge(affine_done.sem, affine_done.at(prev, (1, 3 if l == 0 else 1, NT - 1)))
                    g_, b_ = (ln_w, ln_b) if l == 0 else (ln_a, ln_b2)
                    sp.dma_start(gb[:, 0, :], g_[1:2, :].partition_broadcast(P)).then_inc(gb_in.sem, 16)
                    sp.dma_start(gb[:, 1, :], b_[1:2, :].partition_broadcast(P)).then_inc(gb_in.sem, 16)
                if s == "F" and b == 0:
                    for w in range(3):
                        sp.wait_ge(whi_done[w].sem, whi_done[w].at(w_turn(it, l), l))
                        sp.wait_ge(wlo_done[w].sem, wlo_done[w].at(w_turn(it, l), l))
                        load_w(w, nxt, it)
                if s == "H" and b == 1:
                    if l in SOFT:
                        sp.wait_ge(hs_done.sem, hs_done.at(it, (1, l, NT - 1)))
                    else:
                        sp.wait_ge(biased_done.sem, biased_done.at(it, (1, l, NT - 1)))
                    for w in range(3):
                        if w == 2 or nxt in SOFT:
                            load_bias(w, nxt)
                if s == "R" and l == LAYERS - 1:
                    rows = out[it * 2 + b].rearrange("(t p) d -> p t d", p=P)
                    for h in range(2):
                        half_ = slice(h * NT // 2, (h + 1) * NT // 2)
                        sp.wait_ge(resid_done.sem, resid_done.at(it, (b, l, half_.stop - 1)))
                        sp.dma_start(rows[:, half_, :], n[:, half_, :]).then_inc(stored[b].sem, 16)
                    if not last:
                        load_x(b, it + 1)
                        load_adj(b, it + 1)
                        load_adjt(b, it + 1)

            with sp.Fori(0, PAIRS - 1) as it:
                for s in LOOP:
                    run(*s, it, False)
            for s in LAST:
                run(*s, PAIRS - 1, True)
            for b in range(2):
                sp.wait_ge(stored[b].sem, stored[b].at(PAIRS - 1, "o"))

        @block.tensor
        def _(pe):
            before = {False: occupants(LOOP), True: occupants(LAST)}

            def open_bank(job, it, last):
                if last is not None:
                    (k, b, l, i), turn = before[last][job]
                    s = empties[k] if k != "C" else ctx_done if l in SOFT else ectx_done
                    if not (k == "M" and job[0] in ("UL", "UR")):
                        pe.wait_ge(s.sem, s.at(it - turn, (b, l, i)))
                return bank[bank_of[job]]

            def split_product(dst, terms, ready=None):
                total = 3 * len(terms)
                k = 0
                for n, (shi, slo, rhi, rlo) in enumerate(terms):
                    if ready:
                        ready(n)
                    for a, c in ((shi, rhi), (shi, rlo), (slo, rhi)):
                        ins = pe.matmul(dst, a, c, start=(k == 0), stop=(k == total - 1))
                        k += 1
                return ins

            def wait_h(b, l, it):
                pe.wait_ge(hthi_done.sem, hthi_done.at(h_turn(it, b, l), (b, l, NC - 1)))
                pe.wait_ge(htlo_done.sem, htlo_done.at(h_turn(it, b, l), (b, l, NC - 1)))

            def wait_w(s, l, it):
                pe.wait_ge(whi_done[s].sem, whi_done[s].at(w_turn(it, l), l))
                pe.wait_ge(wlo_done[s].sem, wlo_done[s].at(w_turn(it, l), l))

            def rows_times_w(job, b, t, s, it, last):
                dst = open_bank(job, it, last)
                cols = slice(t * P, (t + 1) * P)
                split_product(dst[:, 0:D], [(hthi[b][:, c, cols], htlo[b][:, c, cols], whi[:, s, c, :], wlo[:, s, c, :])
                                            for c in range(NC)]).then_inc(full[job[0]].sem, 1)

            def run(s, b, l, it, last):
                soft = l in SOFT
                for job in jobs_of(s, b, l):
                    kind, _, _, i = job
                    if kind == "T":
                        if l in (0, 2):
                            pe.wait_ge(xnorm_done.sem, xnorm_done.at(it, (b, l // 2, NT - 1)))
                        else:
                            pe.wait_ge(norm_done.sem, norm_done.at(it, (b, l - 1, NT - 1)))
                        dst = open_bank(job, it, last)
                        for t in range(NT):
                            ins = pe.transpose(dst[:, t * P:(t + 1) * P], n[:, t, i * P:(i + 1) * P], ident[:, :])
                        ins.then_inc(full["T"].sem, 1)
                    if kind == "U":
                        if i == 0:
                            wait_h(b, l, it)
                        cols = slice(i * P, (i + 1) * P)
                        dst = open_bank(job, it, last)
                        split_product(dst[:, :], [(hthi[b][:, c, cols], htlo[b][:, c, cols], hthi[b][:, c, :], htlo[b][:, c, :])
                                                  for c in range(NC)]).then_inc(full["U"].sem, 1)
                    if kind == "M":
                        side, oc = divmod(i, NC)
                        if i == 0:
                            wait_h(b, l, it)
                        if oc == 0:
                            wait_w(side, l, it)
                        cols = slice(oc * P, (oc + 1) * P)
                        dst = open_bank(job, it, last)
                        split_product(dst[:, :], [(whi[:, side, c, cols], wlo[:, side, c, cols], hthi[b][:, c, :], htlo[b][:, c, :])
                                                  for c in range(NC)]).then_inc(full["M"].sem, 1)
                    if kind == "V":
                        side, t = divmod(i, NT) if soft else (2, i)
                        if t == 0:
                            wait_w(side, l, it)
                        rows_times_w(job, b, t, side, it, last)
                    if kind == "HS":
                        if i == 0:
                            wait_w(2, l, it)
                        rows_times_w(job, b, i, 2, it, last)
                    if kind in ("UL", "UR"):
                        side = int(kind == "UR")
                        if i == 0:
                            pe.wait_ge(mhi_done.sem, mhi_done.at(it, (b, l, (side + 1) * NC - 1)))
                            pe.wait_ge(mlo_done.sem, mlo_done.at(it, (b, l, (side + 1) * NC - 1)))
                        cols = slice(i * P, (i + 1) * P)
                        to = slice(0, max((i + 1) * P, MIN_COLS)) if side == 0 else slice(min(i * P, S - MIN_COLS), S)
                        dst = open_bank(job, it, last)
                        split_product(dst[:, to], [(mhi[:, side * NC + c, cols], mlo[:, side * NC + c, cols],
                                                    hthi[b][:, c, to], htlo[b][:, c, to])
                                                   for c in range(NC)]).then_inc(full[kind].sem, 1)
                    if kind == "D":
                        if i == 0:
                            pe.wait_ge(masked_done.sem, masked_done.at(it, (b, l, NT - 1)))
                            pe.wait_ge(upper_done.sem, upper_done.at(it, (b, l, NT - 1)))
                        if i == DIAG:
                            pe.wait_ge(lower_done.sem, lower_done.at(it, (b, l, NT - 1)))
                        dst = open_bank(job, it, last)
                        for t in range(NT):
                            src = lower[:, t, :] if i == DIAG else upper[:, t, :] if t == i else e[:, t, i * P:(i + 1) * P]
                            ins = pe.transpose(dst[:, t * P:(t + 1) * P], src, ident[:, :])
                        ins.then_inc(full["D"].sem, 1)
                    if kind == "C" and soft:
                        cols = slice(i * P, (i + 1) * P)
                        dst = open_bank(job, it, last)
                        pairs = [(j, j) for j in range(i, NT)] + [(DIAG, NT + i)] + [(j, NT + j) for j in range(i)]

                        def parts_ready(k):
                            a = pairs[k][0]
                            pe.wait_ge(dhi_done.sem, dhi_done.at(it, (b, l, a)))
                            pe.wait_ge(dlo_done.sem, dlo_done.at(it, (b, l, a)))
                            if k == 0:
                                pe.wait_ge(vhi_done.sem, vhi_done.at(it, (b, l, 2 * NT - 1)))
                                pe.wait_ge(vlo_done.sem, vlo_done.at(it, (b, l, 2 * NT - 1)))

                        split_product(dst[:, 0:D], [(athi[:, a, cols], atlo[:, a, cols], vhi[:, v, :], vlo[:, v, :])
                                                    for a, v in pairs], parts_ready if i == 0 else None).then_inc(full["C"].sem, 1)
                    if kind == "C" and not soft:
                        cols = slice(i * P, (i + 1) * P)
                        dst = open_bank(job, it, last)

                        def rows_ready(j):
                            pe.wait_ge(ahi_done.sem, ahi_done.at(it, (b, l, j)))
                            pe.wait_ge(alo_done.sem, alo_done.at(it, (b, l, j)))
                            pe.wait_ge(vhi_done.sem, vhi_done.at(it, (b, l, j)))
                            pe.wait_ge(vlo_done.sem, vlo_done.at(it, (b, l, j)))

                        split_product(dst[:, 0:DX], [(athi[:, j, cols], atlo[:, j, cols], linhi[:, j, :], linlo[:, j, :])
                                                     for j in range(NT)], rows_ready if i == 0 else None).then_inc(full["C"].sem, 1)

            pe.wait_ge(masks_done, 3)
            pe.wait_ge(const_done, 3)
            turns(pe, run, full.values())

        def source_of(kind, b, l, i):
            return bank[bank_of[(kind, b, l, i)]]

        @block.scalar
        def _(act):
            def split_w(s, l, it):
                act.wait_ge(w_in[s].sem, w_in[s].at(it, l))
                act.activation(whi[:, s], wraw[:, s], ACT.Copy).then_inc(whi_done[s].sem, 1)

            def value_hi(b, l, i, it):
                dst = vhi[:, i, :] if l in SOFT else linhi[:, i, 0:D]
                act.wait_ge(biased_done.sem, biased_done.at(it, (b, l, i)))
                act.activation(dst, biased[:, biased_done.index[(b, l, i)] % RING, :], ACT.Copy).then_inc(vhi_done.sem, 1)

            def att_hi(b, l, t, it):
                act.wait_ge(weighted_done.sem, weighted_done.at(it, (b, l, t)))
                act.activation(athi[:, t, :], e[:, t, :], ACT.Copy).then_inc(ahi_done.sem, 1)

            def run(s, b, l, it, last):
                soft = l in SOFT
                if s == "Z":
                    ph = l
                    act.wait_ge(xoff_done.sem, xoff_done.at(it, (b, ph)))
                    if ph == 0:
                        if last is not None and b == 1:
                            act.wait_ge(relu_done.sem, relu_done.at(it - 1, (0, 0, NC - 1)))
                        if last is not None:
                            act.wait_ge(stored[b].sem, stored[b].at(it - b, "o"))
                    for t in range(NT):
                        act.activation(n[:, t, :], xs[b][:, t, :], ACT.Identity, bias=xvec["off"][:, b, ph, t:t + 1],
                                       scale=xvec["root"][:, b, ph, t:t + 1]).then_inc(xnorm_done.sem, 1)
                if s == "T":
                    for c in range(NC):
                        act.wait_ge(full["T"].sem, full["T"].at(it, (b, l, c)))
                        act.wait_ge(hthi_done.sem, hthi_done.at(it, (b, l, c), HRING))
                        act.wait_ge(htlo_done.sem, htlo_done.at(it, (b, l, c), HRING))
                        if l % 2:
                            g = l // 2
                            act.activation(htf[:, relu_done.index[(b, l, c)] % HRING, :], source_of("T", b, l, c)[:, :], ACT.Relu, bias=gbt[:, g, 1, c:c + 1],
                                           scale=gbt[:, g, 0, c:c + 1]).then_inc(relu_done.sem, 1)
                        else:
                            act.activation(htf[:, relu_done.index[(b, l, c)] % HRING, :], source_of("T", b, l, c)[:, :], ACT.Relu).then_inc(relu_done.sem, 1)
                if s == "E" and not soft:
                    for i in range(2 * NC):
                        act.wait_ge(full["M"].sem, full["M"].at(it, (b, l, i)))
                        act.activation(mhi[:, i, :], source_of("M", b, l, i)[:, :], ACT.Copy).then_inc(mhi_done.sem, 1)
                if s == "E" and soft:
                    for t in range(NT):
                        act.wait_ge(nmax_done.sem, nmax_done.at(it, (b, l, t)))
                        if t == 0:
                            act.wait_ge(diag_done.sem, diag_done.at(it, (b, l, 0), 1))
                            act.wait_ge(alo_done.sem, alo_done.at(it - 1, (1, 3, NT - 1)))
                        act.activation(e[:, t, :], source_of("U", b, l, t)[:, :], ACT.Exp, bias=vecs["nmax"][:, b, l, t:t + 1],
                                       scale=SCALE, accum_out=vecs["esum"][:, b, l, t:t + 1]).then_inc(exp_done.sem, 1)
                if s == "F" and soft:
                    for i in range(2 * NT):
                        value_hi(b, l, i, it)
                if s == "F" and not soft:
                    value_hi(b, l, 0, it)
                    for t in range(NT):
                        act.wait_ge(scores_done.sem, scores_done.at(it, (b, l, t)))
                        act.activation(e[:, t, :], e[:, t, :], ACT.Exp, scale=SCALE).then_inc(exp_done.sem, 1)
                        if t > 0:
                            att_hi(b, l, t - 1, it)
                if s == "H" and not soft:
                    value_hi(b, l, 1, it)
                    att_hi(b, l, NT - 1, it)
                    for t in range(2, NT):
                        value_hi(b, l, t, it)
                if s == "D" and soft:
                    for i in range(NT + 1):
                        act.wait_ge(full["D"].sem, full["D"].at(it, (b, l, i)))
                        act.activation(athi[:, i, :], source_of("D", b, l, i)[:, :], ACT.Copy).then_inc(dhi_done.sem, 1)
                if s == "K":
                    if b == 1:
                        k, i = ("HS", NT - 1) if soft else ("V", NT - 1)
                        act.wait_ge(full[k].sem, full[k].at(it, (b, l, i)))
                        for w in range(3):
                            split_w(w, (l + 1) % LAYERS, it)
                    if last and (b, l) == (1, 3):
                        act.wait_ge(stored[0].sem, stored[0].at(it, "o"))
                    if not soft:
                        for t in range(NT):
                            act.wait_ge(rrec_done.sem, rrec_done.at(it, (b, l, t)))
                            act.activation(n[:, t, :], source_of("C", b, l, t)[:, 0:D], ACT.Copy,
                                           scale=vecs["rec"][:, b, l, t:t + 1]).then_inc(ectx_done.sem, 1)
                    act.wait_ge(off_done.sem, off_done.at(it, (b, l, 0)))
                    for t in range(NT):
                        act.activation(n[:, t, :], n[:, t, :], ACT.Identity, bias=vecs["off"][:, b, l, t:t + 1],
                                       scale=vecs["rs"][:, b, l, t:t + 1]).then_inc(norm_done.sem, 1)

            act.wait_ge(gbt_in, 16)
            turns(act, run, [relu_done, exp_done, vhi_done, dhi_done, mhi_done, ahi_done, ectx_done, norm_done, xnorm_done, *whi_done], split_w)

        @block.vector
        def _(dve):
            def add_bias(b, l, i, it):
                slot = i // NT if l in SOFT else 2
                dve.wait_ge(full["V"].sem, full["V"].at(it, (b, l, i)))
                if i % NT == 0:
                    dve.wait_ge(bias_in[slot].sem, bias_in[slot].at(w_turn(it, l), l))
                dve.wait_ge(vhi_done.sem, vhi_done.at(it, (b, l, i), RING))
                dve.wait_ge(vlo_done.sem, vlo_done.at(it, (b, l, i), RING))
                dve.tensor_tensor(biased[:, biased_done.index[(b, l, i)] % RING, :], source_of("V", b, l, i)[:, 0:D],
                                  bias[:, slot, :], ALU.add).then_inc(biased_done.sem, 1)

            def att_lo(b, l, t, it):
                dve.wait_ge(ahi_done.sem, ahi_done.at(it, (b, l, t)))
                dve.tensor_tensor(atlo[:, t, :], e[:, t, :], athi[:, t, :].bitcast(F32), ALU.subtract).then_inc(alo_done.sem, 1)

            def weigh(b, l, t, it):
                dve.wait_ge(exp_done.sem, exp_done.at(it, (b, l, t)))
                dve.tensor_tensor(e[:, t, :], e[:, t, :], adjt[b][:, t, :], ALU.mult).then_inc(weighted_done.sem, 1)

            def norm_x(b, ph, it):
                for t in range(NT):
                    dve.bn_stats(stats[:, t, :], xs[b][:, t, :]).then_inc(xstats_done.sem, 1)
                dve.wait_ge(xstats_done.sem, xstats_done.at(it, (b, ph, NT - 1)))
                dve.tensor_copy(carrier[:, :], stats[:, NT - 1, 0:1])
                for t in range(NT):
                    dve.bn_aggr(xmv[:, b, ph, t, :], stats[:, t, :]).then_inc(xaggr_done.sem, 1)
                dve.wait_ge(xaggr_done.sem, xaggr_done.at(it, (b, ph, NT - 1)))
                dve.tensor_scalar(xvec["va"][:, b, ph, :], xmv[:, b, ph, :, 1], NORM_EPS, None, ALU.add).then_inc(xva_done.sem, 1)

            def offset_x(b, ph, it):
                dve.wait_ge(xroot_done.sem, xroot_done.at(it, (b, ph)))
                dve.scalar_tensor_tensor(out=xvec["off"][:, b, ph, :], in0=xmv[:, b, ph, :, 0], scalar=-1.0,
                                         in1=xvec["root"][:, b, ph, :], op0=ALU.mult, op1=ALU.mult).then_inc(xoff_done.sem, 1)

            def run(s, b, l, it, last):
                soft = l in SOFT
                v = {k: t[:, b, l, :] for k, t in vecs.items()}
                if s == "X":
                    dve.wait_ge(x_in[b].sem, x_in[b].at(it - b, "x"))
                    norm_x(b, 0, it)
                if s == "T":
                    for c in range(NC):
                        dve.wait_ge(relu_done.sem, relu_done.at(it, (b, l, c)))
                        dve.tensor_copy(hthi[b][:, c, :], htf[:, relu_done.index[(b, l, c)] % HRING, :]).then_inc(hthi_done.sem, 1)
                if s == "E" and soft:
                    for t in range(NT):
                        dve.wait_ge(full["U"].sem, full["U"].at(it, (b, l, t)))
                        dve.tensor_reduce(v["rmax"][:, t:t + 1], source_of("U", b, l, t)[:, :], AX_X, ALU.max).then_inc(max_done.sem, 1)
                        dve.wait_ge(max_done.sem, max_done.at(it, (b, l, t)))
                        dve.tensor_scalar(v["nmax"][:, t:t + 1], v["rmax"][:, t:t + 1], -SCALE, None, ALU.mult).then_inc(nmax_done.sem, 1)
                if s == "E" and not soft:
                    for i in range(2 * NC):
                        dve.wait_ge(mhi_done.sem, mhi_done.at(it, (b, l, i)))
                        dve.tensor_tensor(mlo[:, i, :], source_of("M", b, l, i)[:, :], mhi[:, i, :].bitcast(F32),
                                          ALU.subtract).then_inc(mlo_done.sem, 1)
                if s == "F" and soft:
                    if l == 0:
                        dve.wait_ge(adj_in[b].sem, adj_in[b].at(it - 1, "a"))
                    for i in range(2 * NT):
                        add_bias(b, l, i, it)
                        if i < NT:
                            dve.wait_ge(exp_done.sem, exp_done.at(it, (b, l, i)))
                            dve.tensor_tensor_reduce(e[:, i, :], e[:, i, :], adjs[b][:, i, :], 1.0, 0.0, ALU.mult, ALU.add,
                                                     v["dsum"][:, i:i + 1]).then_inc(masked_done.sem, 1)
                        else:
                            t = i - NT
                            dve.wait_ge(masked_done.sem, masked_done.at(it, (b, l, t)))
                            dve.wait_ge(diag_done.sem, diag_done.at(it, (b, l, t), 1))
                            dve.tensor_tensor_reduce(diag_scratch[:, :], e[:, t, t * P:(t + 1) * P], ident[:, :], 1.0, 0.0,
                                                     ALU.mult, ALU.add, v["diag"][:, t:t + 1]).then_inc(diag_done.sem, 1)
                            dve.tensor_tensor(lower[:, t, :], e[:, t, t * P:(t + 1) * P], m_lo[:, :], ALU.mult).then_inc(lower_done.sem, 1)
                    dve.scalar_tensor_tensor(out=v["den"], in0=v["esum"], scalar=ATT_EPS, in1=v["dsum"],
                                             op0=ALU.mult, op1=ALU.add).then_inc(den_done.sem, 1)
                    dve.wait_ge(den_done.sem, den_done.at(it, (b, l, 0)))
                    dve.reciprocal(v["rec"], v["den"]).then_inc(rec_done.sem, 1)
                    dve.wait_ge(rec_done.sem, rec_done.at(it, (b, l, 0)))
                    dve.tensor_tensor(v["rec2"], v["rec"], v["rec"], ALU.mult).then_inc(rec2_done.sem, 1)
                if s == "F" and not soft:
                    add_bias(b, l, 0, it)
                    if l == 2:
                        dve.wait_ge(adjr_done.sem, adjr_done.at(it, (b, l, 0)))
                    dve.wait_ge(adjl2_done.sem, adjl2_done.at(it, (b, l, 0)))
                    for t in range(NT):
                        lo = t * P
                        dve.wait_ge(full["UL"].sem, full["UL"].at(it, (b, l, t)))
                        if t == 0:
                            dve.wait_ge(ahi_done.sem, ahi_done.at(it, (b, l, 0), 1))
                        if t > 0:
                            dve.tensor_tensor(e[:, t, 0:lo], source_of("UL", b, l, t)[:, 0:lo], adjt[b][:, t, 0:lo], ALU.mult)
                        dve.tensor_tensor(lower[:, t, :], source_of("UL", b, l, t)[:, lo:lo + P], upper[:, t, :],
                                          ALU.mult).then_inc(left_done.sem, 1)
                        dve.wait_ge(full["UR"].sem, full["UR"].at(it, (b, l, t)))
                        dve.tensor_tensor(e[:, t, lo:S], source_of("UR", b, l, t)[:, lo:S], adjs[b][:, t, lo:S],
                                          ALU.mult).then_inc(right_done.sem, 1)
                        if t >= 1:
                            weigh(b, l, t - 1, it)
                        if t >= 2:
                            att_lo(b, l, t - 2, it)
                if s == "H" and soft:
                    dve.wait_ge(bias_in[2].sem, bias_in[2].at(w_turn(it, l), l))
                    for t in range(NT):
                        dve.wait_ge(full["HS"].sem, full["HS"].at(it, (b, l, t)))
                        dve.tensor_tensor(hs[:, t, :], source_of("HS", b, l, t)[:, 0:D], bias[:, 2, :], ALU.add).then_inc(hs_done.sem, 1)
                if s == "H" and not soft:
                    add_bias(b, l, 1, it)
                    weigh(b, l, NT - 1, it)
                    att_lo(b, l, NT - 2, it)
                    add_bias(b, l, 2, it)
                    att_lo(b, l, NT - 1, it)
                    add_bias(b, l, 3, it)
                if s == "D" and soft:
                    for i in range(NT + 1):
                        dve.wait_ge(dhi_done.sem, dhi_done.at(it, (b, l, i)))
                        dve.tensor_tensor(atlo[:, i, :], source_of("D", b, l, i)[:, :], athi[:, i, :].bitcast(F32),
                                          ALU.subtract).then_inc(dlo_done.sem, 1)
                if s == "K":
                    if soft:
                        dve.wait_ge(hs_done.sem, hs_done.at(it, (b, l, NT - 1)))
                        dve.wait_ge(diag_done.sem, diag_done.at(it, (b, l, NT - 1)))
                    for t in range(NT):
                        dve.wait_ge(full["C"].sem, full["C"].at(it, (b, l, t)))
                        if soft:
                            dve.scalar_tensor_tensor(out=n[:, t, :], in0=hs[:, t, :], scalar=v["diag"][:, t:t + 1],
                                                     in1=source_of("C", b, l, t)[:, 0:D], op0=ALU.mult, op1=ALU.add).then_inc(ctx_done.sem, 1)
                            dve.wait_ge(ctx_done.sem, ctx_done.at(it, (b, l, t)))
                        else:
                            dve.tensor_scalar(v["den"][:, t:t + 1], source_of("C", b, l, t)[:, D:D + 1], ATT_EPS, None,
                                              ALU.add).then_inc(rsum_done.sem, 1)
                            dve.wait_ge(rsum_done.sem, rsum_done.at(it, (b, l, t)))
                            dve.reciprocal(v["rec"][:, t:t + 1], v["den"][:, t:t + 1]).then_inc(rrec_done.sem, 1)
                            dve.wait_ge(ectx_done.sem, ectx_done.at(it, (b, l, t)))
                        dve.bn_stats(stats[:, t, :], n[:, t, :]).then_inc(stats_done.sem, 1)
                    dve.wait_ge(stats_done.sem, stats_done.at(it, (b, l, NT - 1)))
                    dve.tensor_copy(carrier[:, :], stats[:, NT - 1, 0:1])
                    for t in range(NT):
                        dve.bn_aggr(mv[:, b, l, t, :], stats[:, t, :]).then_inc(aggr_done.sem, 1)
                    dve.wait_ge(aggr_done.sem, aggr_done.at(it, (b, l, NT - 1)))
                    mean, var = mv[:, b, l, :, 0], mv[:, b, l, :, 1]
                    if soft:
                        dve.tensor_tensor(v["va"], var, v["rec2"], ALU.mult).then_inc(va_done.sem, 1)
                        dve.wait_ge(va_done.sem, va_done.at(it, (b, l, 0)))
                        dve.tensor_scalar(v["vb"], v["va"], SOFT_EPS, None, ALU.add).then_inc(vb_done.sem, 1)
                        dve.wait_ge(root_done.sem, root_done.at(it, (b, l, 0)))
                        dve.tensor_tensor(v["rs"], v["root"], v["rec"], ALU.mult).then_inc(rs_done.sem, 1)
                    else:
                        dve.tensor_scalar(v["va"], var, float(D) / (D - 1), None, ALU.mult).then_inc(va_done.sem, 1)
                        dve.wait_ge(root_done.sem, root_done.at(it, (b, l, 0)))
                        dve.tensor_scalar(v["vb"], v["root"], EXP_EPS, None, ALU.add).then_inc(eps_done.sem, 1)
                        dve.wait_ge(eps_done.sem, eps_done.at(it, (b, l, 0)))
                        dve.reciprocal(v["rs"], v["vb"]).then_inc(rs_done.sem, 1)
                    dve.wait_ge(rs_done.sem, rs_done.at(it, (b, l, 0)))
                    dve.scalar_tensor_tensor(out=v["off"], in0=mean, scalar=-1.0, in1=v["rs"],
                                             op0=ALU.mult, op1=ALU.mult).then_inc(off_done.sem, 1)
                if s == "R":
                    dve.wait_ge(gb_in.sem, gb_in.at(it, l))
                    for t in range(NT):
                        dve.wait_ge(norm_done.sem, norm_done.at(it, (b, l, t)))
                        dve.tensor_tensor(n[:, t, :], n[:, t, :], gb[:, 0, :], ALU.mult).then_inc(gain_done.sem, 1)
                    for t in range(NT):
                        dve.wait_ge(affine_done.sem, affine_done.at(it, (b, l, t)))
                        dst = xs[b] if l == 1 else n
                        dve.scalar_tensor_tensor(out=dst[:, t, :], in0=n[:, t, :], scalar=0.0, in1=xs[b][:, t, :],
                                                 op0=ALU.max, op1=ALU.add).then_inc(resid_done.sem, 1)
                if s == "N":
                    dve.wait_ge(resid_done.sem, resid_done.at(it, (b, 1, NT - 1)))
                    norm_x(b, 1, it)
                if s == "Z":
                    offset_x(b, l, it)

            dve.memset(half[:, 0, :], 0.5).then_inc(const_done, 1)
            dve.memset(half[:, 1, :], -0.5).then_inc(const_done, 1)
            dve.memset(linhi[:, :, D:DX].bitcast(F32), 1.0).then_inc(const_done, 1)
            dve.memset(linlo[:, :, D:DX].bitcast(F32), 0.0).then_inc(const_done, 1)
            dve.wait_ge(masks_done, 3)
            turns(dve, run, [hthi_done, max_done, nmax_done, masked_done, diag_done, lower_done, den_done, rec_done, rec2_done, biased_done,
                             hs_done, dlo_done, mlo_done, right_done, left_done, weighted_done, gain_done, alo_done, rsum_done, rrec_done, ctx_done,
                             stats_done, aggr_done, va_done, vb_done, eps_done, rs_done, off_done, resid_done,
                             xstats_done, xaggr_done, xva_done, xoff_done])

        @block.gpsimd
        def _(pool):
            def split_w(s, l, it):
                pool.wait_ge(whi_done[s].sem, whi_done[s].at(it, l))
                pool.tensor_tensor(wlo[:, s], wraw[:, s], whi[:, s].bitcast(F32), ALU.subtract).then_inc(wlo_done[s].sem, 1)

            def value_lo(b, l, i, it):
                hi, dst = (vhi[:, i, :], vlo[:, i, :]) if l in SOFT else (linhi[:, i, 0:D], linlo[:, i, 0:D])
                pool.wait_ge(vhi_done.sem, vhi_done.at(it, (b, l, i)))
                pool.tensor_tensor(dst, biased[:, biased_done.index[(b, l, i)] % RING, :], hi.bitcast(F32),
                                   ALU.subtract).then_inc(vlo_done.sem, 1)

            def diagonal(a):
                v = a[:, :, :].rearrange("p t s -> p (t s)")
                return [v[:, t * (S + P):t * (S + P) + P] for t in range(NT)]

            def run(s, b, l, it, last):
                soft = l in SOFT
                if s == "T":
                    for c in range(NC):
                        pool.wait_ge(hthi_done.sem, hthi_done.at(it, (b, l, c)))
                        pool.tensor_tensor(htlo[b][:, c, :], htf[:, relu_done.index[(b, l, c)] % HRING, :], hthi[b][:, c, :].bitcast(F32),
                                           ALU.subtract).then_inc(htlo_done.sem, 1)
                if s == "F" and soft:
                    for i in range(2 * NT):
                        value_lo(b, l, i, it)
                        if i >= NT:
                            t = i - NT
                            pool.wait_ge(masked_done.sem, masked_done.at(it, (b, l, t)))
                            pool.tensor_tensor(upper[:, t, :], diagonal(e)[t], m_up[:, :], ALU.mult).then_inc(upper_done.sem, 1)
                if s == "E" and not soft:
                    if l == 2:
                        pool.wait_ge(masked_done.sem, masked_done.at(it, (b, 1, NT - 1)))
                        for blk in diagonal(adjs[b]):
                            ins = pool.tensor_tensor(blk, blk, m_up[:, :], ALU.mult)
                        ins.then_inc(adjr_done.sem, 1)
                        pool.wait_ge(adjt_in[b].sem, adjt_in[b].at(it - 1, "a"))
                    pool.wait_ge(left_done.sem, left_done.at(it, (b, l, 0), 1))
                    if l == 2 and b == 0:
                        pool.wait_ge(full["D"].sem, full["D"].at(it, (1, 1, NT)))
                    for t, blk in enumerate(diagonal(adjt[b])):
                        ins = pool.tensor_tensor(upper[:, t, :], blk, m_up[:, :], ALU.mult)
                    ins.then_inc(adjl_done.sem, 1)
                    pool.wait_ge(adjl_done.sem, adjl_done.at(it, (b, l, 0)))
                    for t, blk in enumerate(diagonal(adjt[b])):
                        ins = pool.tensor_tensor(upper[:, t, :], blk, upper[:, t, :], ALU.subtract)
                    ins.then_inc(adjl2_done.sem, 1)
                if s == "F" and not soft:
                    value_lo(b, l, 0, it)
                    for t in range(NT):
                        blk = diagonal(e)[t]
                        pool.wait_ge(right_done.sem, right_done.at(it, (b, l, t)))
                        pool.tensor_tensor(blk, blk, lower[:, t, :], ALU.add).then_inc(scores_done.sem, 1)
                if s == "H" and not soft:
                    for t in range(1, NT):
                        value_lo(b, l, t, it)
                if s == "K":
                    if b == 1:
                        split_w(0, (l + 1) % LAYERS, it)
                        split_w(1, (l + 1) % LAYERS, it)
                    src = vb_done if soft else va_done
                    pool.wait_ge(src.sem, src.at(it, (b, l, 0)))
                    pool.tensor_tensor(vecs["root"][:, b, l, :], vecs["vb" if soft else "va"][:, b, l, :],
                                       half[:, 1 if soft else 0, :], ALU.pow).then_inc(root_done.sem, 1)
                    if b == 1:
                        split_w(2, (l + 1) % LAYERS, it)
                if s == "R":
                    pool.wait_ge(gb_in.sem, gb_in.at(it, l))
                    for t in range(NT):
                        pool.wait_ge(gain_done.sem, gain_done.at(it, (b, l, t)))
                        pool.tensor_tensor(n[:, t, :], n[:, t, :], gb[:, 1, :], ALU.add).then_inc(affine_done.sem, 1)
                if s in "XN":
                    ph = 0 if s == "X" else 1
                    pool.wait_ge(xva_done.sem, xva_done.at(it, (b, ph)))
                    pool.tensor_tensor(xvec["root"][:, b, ph, :], xvec["va"][:, b, ph, :], half[:, 1, :],
                                       ALU.pow).then_inc(xroot_done.sem, 1)

            for m in (ident, m_up, m_lo):
                pool.memset(m[:, :], 1.0).then_inc(mask_step, 1)
            pool.wait_ge(mask_step, 3)
            for m, op, sign in ((ident, ALU.is_equal, 1), (m_up, ALU.is_gt, 1), (m_lo, ALU.is_gt, -1)):
                pool.affine_select(out=m[:, :], in_=m[:, :], compare_op=op, fill=0.0, base=0,
                                   pattern=[[sign, P]], channel_multiplier=-sign).then_inc(masks_done, 1)
            pool.wait_ge(masks_done, 3)
            pool.wait_ge(const_done, 4)
            turns(pool, run, [htlo_done, upper_done, vlo_done, adjr_done, adjl_done, adjl2_done, scores_done,
                              root_done, affine_done, xroot_done, *wlo_done], split_w)


_NAMES = ["L0_gnn_Wl", "L0_gnn_bl", "L0_gnn_Ws", "L0_gnn_bs", "L0_gnn_Wr", "L0_gnn_br", "L0_gnn_ln_w", "L0_gnn_ln_b",
          "L1_gnn_W_left", "L1_gnn_W_right", "L1_gnn_W_lin", "L1_gnn_b_lin", "L1_gnn_ln_a", "L1_gnn_ln_b"]


def kernel(**inputs):
    import numpy as _np
    import concourse.bacc as _bacc
    from concourse import mybir as _mybir
    from concourse.bass_utils import run_bass_kernel_spmd as _run

    nc = _bacc.Bacc("TRN2", target_bir_lowering=False, num_devices=1)
    arrays, args = {}, []

    def give(name, a):
        a = _np.ascontiguousarray(a)
        arrays[f"in_{name}_dram"] = a
        args.append(nc.dram_tensor(f"in_{name}_dram", a.shape, _mybir.dt.from_np(a.dtype), kind="ExternalInput").ap())

    x = _np.asarray(inputs["x"])
    adj = _np.asarray(inputs["adj"])
    give("x", x)
    give("adj", adj)
    give("adj_t", adj.transpose(0, 2, 1))
    for name in _NAMES:
        a = _np.asarray(inputs[name])
        give(name, a.transpose(0, 2, 1) if a.ndim == 3 else a)
    norms = _np.stack([_np.asarray(inputs[k])[0] for k in ("L0_gnn_ln_w", "L0_gnn_ln_b", "L1_gnn_ln_a", "L1_gnn_ln_b")])
    give("norm_t", norms.reshape(2, 2, -1, P).transpose(3, 0, 1, 2))
    out = nc.dram_tensor("out_0_dram", x.shape, _mybir.dt.float32, kind="ExternalOutput").ap()
    program(nc, *args, out)
    r = _run(nc, [arrays], core_ids=[0])
    return r.results[0]["out_0_dram"]
```

```python
from contextlib import ExitStack

import concourse.bass as bass
from concourse import mybir

ALU = mybir.AluOpType
ACT = mybir.ActivationFunctionType
AX_X = mybir.AxisListType.X
F32 = mybir.dt.float32
F32R = mybir.dt.float32r

P = 128
LAYERS = 4
SOFT, EXPL, BOTH = (0, 1), (2, 3), (0, 1, 2, 3)
NORM_EPS, ATT_EPS, SOFT_EPS, EXP_EPS = 1e-5, 1e-10, 1e-12, 1e-3
MIN_COLS = 256


def sections(last):
    out = []
    for l in range(LAYERS):
        nxt, none_next = (l + 1) % LAYERS, last and l == LAYERS - 1
        ends = [[("L", b, l)] + [("R", b, l)] * (l % 2) for b in range(2)]
        out += [("E", 0, l)] * (l in EXPL) + [("N", 1, 1), ("Z", 1, 1)] * (l == 2)
        out += [("F", 0, l)] + [("X", 1, 0)] * (l == 0) + [("H", 0, l)] + [("Z", 1, 0)] * (l == 0)
        out += [("D", 0, l), ("T", 1, l), ("K", 0, l)]
        out += [("E", 1, l)] + ends[0] if l in SOFT else ends[0] + [("E", 1, l)]
        out += [("F", 1, l)] + [("X", 0, 0), ("Z", 0, 0)] * (l == LAYERS - 1 and not last) + [("N", 0, 1)] * (l == 1)
        out += [("H", 1, l)] + [("Z", 0, 1)] * (l == 1) + [("D", 1, l)]
        out += [("T", 0, nxt)] * (not none_next) + [("K", 1, l)] + [("E", 0, nxt)] * (nxt in SOFT and not none_next) + ends[1]
    return out


AHEAD = [("X", 0, 0), ("Z", 0, 0), ("T", 0, 0), ("E", 0, 0)]

BESIDE = {(0, 0): (1, 0), (1, 1): (0, 1), (1, LAYERS - 1): (0, 0)}


class Signal:

    def __init__(self, ctx, nc, name, keys, step=1, ahead=0):
        self.sem = ctx.enter_context(nc.semaphore(name))
        self.index = {k: n for n, k in enumerate(keys)}
        assert len(self.index) == len(keys)
        self.turn, self.step, self.ahead = len(keys), step, ahead

    def credit(self, eng):
        if self.turn > self.ahead:
            eng.sem_inc(self.sem, (self.turn - self.ahead) * self.step)

    def at(self, it, key, back=0):
        return (it + 1) * (self.turn * self.step) + (self.index[key] + 1 - back) * self.step


def program(nc, x, adj, adj_t, wl, bl, ws, bs, wr, br, ln_w, ln_b, w_left, w_right, w_lin, b_lin, ln_a, ln_b2, norm_t, out):
    G, S, D = x.shape
    NT, NC, PAIRS = S // P, D // P, G // 2
    DX = D + 2
    SCALE = float(D) ** -0.5
    LOOP, LAST = sections(False), sections(True)
    HALVES = [slice(0, NT // 2), slice(NT // 2, NT)]
    AFTER = 1
    DIAG = NT

    def keys(section, layers, n, loop=LOOP):
        return [(b, l, i) for s, b, l in loop if s == section and l in layers for i in range(n)]

    def jobs_of(s, b, l):
        soft = l in SOFT
        if s == "T":
            return [("T", b, l, c) for c in range(NC)]
        if s == "E" and soft:
            return [("U", b, l, t) for t in range(NT)]
        if s == "E":
            return [("M", b, l, i) for i in range(2 * NC)]
        if s == "F" and soft:
            return [("V", b, l, i) for i in range(2 * NT)]
        if s == "F":
            return [("V", b, l, 0)] + [(k, b, l, t) for t in range(NT) for k in ("UL", "UR")]
        if s == "H" and soft:
            return [("HS", b, l, t) for t in range(NT)]
        if s == "H":
            return [("V", b, l, t) for t in range(1, NT)]
        if s == "D":
            return [("D", b, l, i) for i in range(NT + 1) if soft]
        if s == "K":
            return [("C", b, l, t) for t in range(NT)]
        return []

    jobs = [j for s in LOOP for j in jobs_of(*s)]
    skip = jobs.index(("HS", 0, 1, 0))
    bank_of = {j: (n + (n >= skip) * (-len(jobs) % 8)) % 8 for n, j in enumerate(jobs)}

    def occupants(order):
        held, before = {}, {}
        for turn in (0, 1):
            for j in [j for s in (LOOP if turn == 0 else order) for j in jobs_of(*s)]:
                before[j] = held.get(bank_of[j])
                held[bank_of[j]] = (j, turn)
        return {j: (k[0], 1 - k[1]) for j, k in before.items() if k}

    ROW_KEYS = [(b, l, t) for s, b, l in LOOP if l in SOFT and s in "EF" for t in ([0] if s == "E" else range(1, NT))]
    V_KEYS = [(b, l, i) for k, b, l, i in jobs if k == "V"]

    with ExitStack() as ctx:
        def sb(name, shape, dt=F32):
            return ctx.enter_context(nc.sbuf_tensor(name, shape, dt))

        def signal(name, k, step=1, ahead=0):
            return Signal(ctx, nc, name, k, step, ahead)

        bank = [ctx.enter_context(nc.psum_tensor(f"bank{i}", [P, 512], F32)) for i in range(8)]

        xs = [sb(f"x{b}", [P, NT, D]) for b in range(2)]
        adjs = [sb(f"adj{b}", [P, NT, S]) for b in range(2)]
        adjt = [sb(f"adjT{b}", [P, NT, S]) for b in range(2)]
        hthi = [sb(f"hThi{b}", [P, NC, S], F32R) for b in range(2)]
        htlo = [sb(f"hTlo{b}", [P, NC, S], F32R) for b in range(2)]
        HRING = 2
        n = sb("n", [P, NT, D])
        htf = sb("hTf", [P, HRING, S])
        e = sb("e", [P, NT, S])
        upper = sb("upper", [P, NT, P])
        lower = sb("lower", [P, NT, P])
        athi = sb("attThi", [P, NT + 1, S], F32R)
        atlo = sb("attTlo", [P, NT + 1, S], F32R)
        vhi = sb("vhi", [P, 2 * NT, D], F32R)
        vlo = sb("vlo", [P, 2 * NT, D], F32R)
        mhi = vhi[:, :, :].rearrange("p a b -> p (a b)").rearrange("p (m s) -> p m s", s=S)
        mlo = vlo[:, :, :].rearrange("p a b -> p (a b)").rearrange("p (m s) -> p m s", s=S)
        linhi = sb("linhi", [P, NT, DX], F32R)
        linlo = sb("linlo", [P, NT, DX], F32R)
        hs = sb("hs", [P, NT, D])
        RING = 2
        biased = sb("biased", [P, RING, D])
        whi = sb("whi", [P, 3, NC, D], F32R)
        wlo = sb("wlo", [P, 3, NC, D], F32R)
        wraw = sb("wraw", [P, 3, NC, D])
        bias = sb("bias", [P, 3, D])
        gb = sb("gb", [P, 2, D])
        gbt = sb("gbT", [P, 2, 2, NC])
        ident = sb("ident", [P, P])
        m_up = sb("m_up", [P, P])
        m_lo = sb("m_lo", [P, P])
        half = sb("half", [P, 2, NT])
        stats = sb("stats", [P, NT, 6])
        carrier = sb("carrier", [P, 1])
        diag_scratch = sb("diag_scratch", [P, P])
        mv = sb("mv", [P, 2, LAYERS, NT, 2])
        vecs = {k: sb(k, [P, 2, LAYERS, NT]) for k in
                ("rmax", "nmax", "esum", "dsum", "diag", "den", "rec", "rec2", "va", "vb", "root", "rs", "off")}
        xmv = sb("xmv", [P, 2, 2, NT, 2])
        xvec = {k: sb("x" + k, [P, 2, 2, NT]) for k in ("va", "root", "off")}

        x_in = [[signal(f"x_in{b}_{h}", ["x"], 16, 1) for h in range(2)] for b in range(2)]
        adj_in = [signal(f"adj_in{b}", ["a"], 16, 1) for b in range(2)]
        adjt_in = [signal(f"adjT_in{b}", ["a"], 16, 1) for b in range(2)]
        w_in = [signal(f"w_in{s}", [1, 2, 3, 0], 16, 1) for s in range(3)]
        bias_in = [signal(f"bias_in{s}", [1, 2, 3, 0] if s == 2 else [1, 0], 16, 1) for s in range(3)]
        gb_in = signal("gb_in", [1, 3], 32)
        gbt_in = ctx.enter_context(nc.semaphore("gbT_in"))
        stored = [signal(f"stored{b}", ["o"], 32) for b in range(2)]
        full = {k: signal("full_" + k, ROW_KEYS if k == "U" else [(b, l, i) for kk, b, l, i in jobs if kk == k], 1,
                          {"T": NC, "U": 1}.get(k, 0))
                for k in ("T", "U", "M", "V", "HS", "D", "C", "UL", "UR")}
        row1_done = signal("row1_done", keys("E", SOFT, 1), 1, 1)
        masks_done = ctx.enter_context(nc.semaphore("masks_done"))
        mask_step = ctx.enter_context(nc.semaphore("mask_step"))
        const_done = ctx.enter_context(nc.semaphore("const_done"))
        relu_done = signal("relu_done", keys("T", BOTH, NC), 1, NC)
        hthi_done = signal("hThi_done", keys("T", BOTH, NC), 1, NC)
        htlo_done = signal("hTlo_done", keys("T", BOTH, NC), 1, NC)
        max_done = signal("max_done", ROW_KEYS, 1, 1)
        nmax_done = signal("nmax_done", ROW_KEYS, 1, 1)
        above_done = signal("above_done", keys("E", SOFT, 2), 1, 2)
        exp_done = signal("exp_done", keys("F", BOTH, NT))
        masked_done = signal("masked_done", keys("F", SOFT, NT))
        diag_done = signal("diag_done", keys("F", SOFT, NT))
        upper_done = signal("upper_done", keys("F", SOFT, NT))
        lower_done = signal("lower_done", keys("F", SOFT, NT))
        den_done = signal("den_done", keys("H", SOFT, 1))
        rec_done = signal("rec_done", keys("H", SOFT, 1))
        rec2_done = signal("rec2_done", keys("H", SOFT, 1))
        biased_done = signal("biased_done", V_KEYS)
        vhi_done = signal("vhi_done", V_KEYS)
        vlo_done = signal("vlo_done", V_KEYS)
        hs_done = signal("hs_done", keys("H", SOFT, NT))
        dhi_done = signal("dhi_done", keys("D", SOFT, NT + 1))
        dlo_done = signal("dlo_done", keys("D", SOFT, NT + 1))
        mhi_done = signal("mhi_done", keys("E", EXPL, 2 * NC))
        mlo_done = signal("mlo_done", keys("E", EXPL, 2 * NC))
        adjr_done = signal("adjR_done", keys("E", (2,), 1))
        adjl_done = signal("adjL_done", keys("E", EXPL, 1))
        adjl2_done = signal("adjL2_done", keys("E", EXPL, 1))
        right_done = signal("right_done", keys("F", EXPL, NT))
        left_done = signal("left_done", keys("F", EXPL, NT))
        scores_done = signal("scores_done", keys("F", EXPL, NT))
        weighted_done = signal("weighted_done", keys("F", EXPL, NT))
        ahi_done = signal("ahi_done", keys("F", EXPL, NT))
        alo_done = signal("alo_done", keys("F", EXPL, NT))
        rsum_done = signal("rsum_done", keys("K", EXPL, NT))
        rrec_done = signal("rrec_done", keys("K", EXPL, NT))
        ctx_done = signal("ctx_done", keys("K", SOFT, NT))
        ectx_done = signal("ectx_done", keys("K", EXPL, NT))
        stats_done = signal("stats_done", keys("K", BOTH, NT))
        aggr_done = signal("aggr_done", keys("K", BOTH, NT))
        va_done = signal("va_done", keys("K", BOTH, 1))
        vb_done = signal("vb_done", keys("K", SOFT, 1))
        root_done = signal("root_done", keys("K", BOTH, 1))
        eps_done = signal("eps_done", keys("K", EXPL, 1))
        rs_done = signal("rs_done", keys("K", BOTH, 1))
        off_done = signal("off_done", keys("K", BOTH, 1))
        norm_done = signal("norm_done", keys("K", BOTH, NT))
        gain_done = signal("gain_done", keys("R", BOTH, NT))
        affine_done = signal("affine_done", keys("R", BOTH, NT))
        resid_done = signal("resid_done", keys("R", BOTH, NT))
        x_keys = [(b, 0 if s == "X" else 1, t) for s, b, l in LOOP if s in "XN" for t in range(NT)]
        x_one = [(b, 0 if s == "X" else 1) for s, b, l in LOOP if s in "XN"]
        z_one = [(b, ph) for s, b, ph in LOOP if s == "Z"]
        xstats_done = signal("xstats_done", x_keys, 1, NT)
        xaggr_done = signal("xaggr_done", x_keys, 1, NT)
        xva_done = signal("xva_done", x_one, 1, 1)
        xroot_done = signal("xroot_done", x_one, 1, 1)
        xoff_done = signal("xoff_done", z_one, 1, 1)
        xnorm_done = signal("xnorm_done", [(*z, t) for z in z_one for t in range(NT)], 1, NT)
        whi_done = [signal(f"whi_done{s}", [1, 2, 3, 0], 1, 1) for s in range(3)]
        wlo_done = [signal(f"wlo_done{s}", [1, 2, 3, 0], 1, 1) for s in range(3)]

        empties = {"T": relu_done, "U": exp_done, "M": mlo_done, "V": biased_done, "HS": hs_done,
                   "D": dlo_done, "UL": left_done, "UR": right_done}

        def w_turn(it, l):
            return it - (l == 0)

        def e_turn(it, b, l):
            return it - ((b, l) == (0, 0))

        def turns(eng, run, own, split_w=None):
            for s in own:
                s.credit(eng)
            for s in AHEAD:
                run(*s, -1, None)
            if split_w:
                for s in range(3):
                    split_w(s, 0, -1)
            with eng.Fori(0, PAIRS - 1) as it:
                for s in LOOP:
                    run(*s, it, False)
            for s in LAST:
                run(*s, PAIRS - 1, True)

        def inlined(b, ph, last):
            return last is not None and (b, ph) in BESIDE.values()

        def beside_of(s, b, l, last):
            return BESIDE.get((b, l)) if s == "F" and not (last and l == LAYERS - 1) else None

        block = ctx.enter_context(nc.Block())

        @block.sync
        def _(sp):
            w_dram = lambda s, l: ((wl, wr, ws) if l < 2 else (w_left, w_right, w_lin))[s][l % 2].rearrange("(c p) o -> p c o", p=P)
            b_dram = lambda s, l: ((bl, br, bs) if l < 2 else (None, None, b_lin))[s][l % 2:l % 2 + 1, :].partition_broadcast(P)

            def load_w(s, l, it):
                sp.dma_start(wraw[:, s], w_dram(s, l)).then_inc(w_in[s].sem, 16)

            def load_bias(s, l):
                sp.dma_start(bias[:, s, :], b_dram(s, l)).then_inc(bias_in[s].sem, 16)

            def load_x(b, pair, h):
                rows = x[pair * 2 + b].rearrange("(t p) d -> p t d", p=P)
                sp.dma_start(xs[b][:, HALVES[h], :], rows[:, HALVES[h], :]).then_inc(x_in[b][h].sem, 16)

            def load_adj(b, pair):
                sp.dma_start(adjs[b][:, :, :], adj[pair * 2 + b].rearrange("(t p) s -> p t s", p=P)).then_inc(adj_in[b].sem, 16)

            def load_adjt(b, pair):
                sp.dma_start(adjt[b][:, :, :], adj_t[pair * 2 + b].rearrange("(t p) s -> p t s", p=P)).then_inc(adjt_in[b].sem, 16)

            for s in (*w_in, *bias_in, gb_in, *stored):
                s.credit(sp)
            for h in range(2):
                load_x(0, 0, h)
            sp.dma_start(gbt[:, :, :, :], norm_t).then_inc(gbt_in, 16)
            load_adj(0, 0)
            for s in range(3):
                load_w(s, 0, -1)
                load_bias(s, 0)
            for h in range(2):
                load_x(1, 0, h)
            load_adj(1, 0)
            load_adjt(0, 0)
            load_adjt(1, 0)

            def run(s, b, l, it, last):
                nxt = (l + 1) % LAYERS
                if s == "F" and b == 0 and l in (0, 2):
                    prev = it - (l == 0)
                    sp.wait_ge(affine_done.sem, affine_done.at(prev, (1, 3 if l == 0 else 1, NT - 1)))
                    g_, b_ = (ln_w, ln_b) if l == 0 else (ln_a, ln_b2)
                    sp.dma_start(gb[:, 0, :], g_[1:2, :].partition_broadcast(P)).then_inc(gb_in.sem, 16)
                    sp.dma_start(gb[:, 1, :], b_[1:2, :].partition_broadcast(P)).then_inc(gb_in.sem, 16)
                if s == "F" and b == 0:
                    for w in range(3):
                        sp.wait_ge(whi_done[w].sem, whi_done[w].at(w_turn(it, l), l))
                        sp.wait_ge(wlo_done[w].sem, wlo_done[w].at(w_turn(it, l), l))
                        load_w(w, nxt, it)
                if s == "H" and b == 1:
                    if l in SOFT:
                        sp.wait_ge(hs_done.sem, hs_done.at(it, (1, l, NT - 1)))
                    else:
                        sp.wait_ge(biased_done.sem, biased_done.at(it, (1, l, NT - 1)))
                    for w in range(3):
                        if w == 2 or nxt in SOFT:
                            load_bias(w, nxt)
                if s == "R" and l == LAYERS - 1:
                    rows = out[it * 2 + b].rearrange("(t p) d -> p t d", p=P)
                    for h, tiles in enumerate(HALVES):
                        sp.wait_ge(resid_done.sem, resid_done.at(it, (b, l, tiles.stop - 1)))
                        sp.dma_start(rows[:, tiles, :], n[:, tiles, :]).then_inc(stored[b].sem, 16)
                        if not last:
                            load_x(b, it + 1, h)
                    if not last:
                        load_adj(b, it + 1)
                        load_adjt(b, it + 1)

            with sp.Fori(0, PAIRS - 1) as it:
                for s in LOOP:
                    run(*s, it, False)
            for s in LAST:
                run(*s, PAIRS - 1, True)
            for b in range(2):
                sp.wait_ge(stored[b].sem, stored[b].at(PAIRS - 1, "o"))

        @block.tensor
        def _(pe):
            before = {False: occupants(LOOP), True: occupants(LAST)}

            def open_bank(job, it, last):
                if last is not None:
                    (k, b, l, i), turn = before[last][job]
                    if (k, b, l) == ("U", 0, 0):
                        turn -= 1
                    s = empties[k] if k != "C" else ctx_done if l in SOFT else ectx_done
                    if not (k == "M" and job[0] in ("UL", "UR")):
                        pe.wait_ge(s.sem, s.at(it - turn, (b, l, i)))
                return bank[bank_of[job]]

            def split_product(dst, terms, ready=None):
                total = 3 * len(terms)
                k = 0
                for n, (shi, slo, rhi, rlo) in enumerate(terms):
                    if ready:
                        ready(n)
                    for a, c in ((shi, rhi), (shi, rlo), (slo, rhi)):
                        ins = pe.matmul(dst, a, c, start=(k == 0), stop=(k == total - 1))
                        k += 1
                return ins

            def wait_h(b, l, it):
                pe.wait_ge(hthi_done.sem, hthi_done.at(it, (b, l, NC - 1)))
                pe.wait_ge(htlo_done.sem, htlo_done.at(it, (b, l, NC - 1)))

            def wait_w(s, l, it):
                pe.wait_ge(whi_done[s].sem, whi_done[s].at(w_turn(it, l), l))
                pe.wait_ge(wlo_done[s].sem, wlo_done[s].at(w_turn(it, l), l))

            def rows_times_w(job, b, t, s, it, last):
                dst = open_bank(job, it, last)
                cols = slice(t * P, (t + 1) * P)
                split_product(dst[:, 0:D], [(hthi[b][:, c, cols], htlo[b][:, c, cols], whi[:, s, c, :], wlo[:, s, c, :])
                                            for c in range(NC)]).then_inc(full[job[0]].sem, 1)

            def complete_scores(b, l, it):
                pe.wait_ge(above_done.sem, above_done.at(e_turn(it, b, l), (b, l, 1)))
                for t in range(1, NT):
                    dst = bank[bank_of[("U", b, l, t)]]
                    for j in range(min(t, NT - 2)):
                        ins = pe.transpose(dst[:, j * P:(j + 1) * P], (upper, lower)[j][:, t - 1 - j, :], ident[:, :])
                    ins.then_inc(full["U"].sem, 1)

            def run(s, b, l, it, last):
                soft = l in SOFT
                for job in jobs_of(s, b, l):
                    kind, _, _, i = job
                    if kind == "T":
                        if l in (0, 2):
                            pe.wait_ge(xnorm_done.sem, xnorm_done.at(it, (b, l // 2, NT - 1)))
                        else:
                            pe.wait_ge(norm_done.sem, norm_done.at(it, (b, l - 1, NT - 1)))
                        dst = open_bank(job, it, last)
                        for t in range(NT):
                            ins = pe.transpose(dst[:, t * P:(t + 1) * P], n[:, t, i * P:(i + 1) * P], ident[:, :])
                        ins.then_inc(full["T"].sem, 1)
                    if kind == "U":
                        if i == 0:
                            wait_h(b, l, it)
                        cols = slice(i * P, (i + 1) * P)
                        to = slice(min(i * P, S - MIN_COLS), S)
                        dst = open_bank(job, it, last)
                        ins = split_product(dst[:, to], [(hthi[b][:, c, cols], htlo[b][:, c, cols], hthi[b][:, c, to], htlo[b][:, c, to])
                                                         for c in range(NC)])
                        if i == 0:
                            ins.then_inc(full["U"].sem, 1)
                        if i == 1:
                            ins.then_inc(row1_done.sem, 1)
                    if kind == "M":
                        side, oc = divmod(i, NC)
                        if i == 0:
                            wait_h(b, l, it)
                        if oc == 0:
                            wait_w(side, l, it)
                        cols = slice(oc * P, (oc + 1) * P)
                        dst = open_bank(job, it, last)
                        split_product(dst[:, :], [(whi[:, side, c, cols], wlo[:, side, c, cols], hthi[b][:, c, :], htlo[b][:, c, :])
                                                  for c in range(NC)]).then_inc(full["M"].sem, 1)
                    if kind == "V":
                        side, t = divmod(i, NT) if soft else (2, i)
                        if soft and i == AFTER:
                            complete_scores(b, l, it)
                        if t == 0:
                            wait_w(side, l, it)
                        rows_times_w(job, b, t, side, it, last)
                    if kind == "HS":
                        if i == 0:
                            wait_w(2, l, it)
                        rows_times_w(job, b, i, 2, it, last)
                    if kind in ("UL", "UR"):
                        side = int(kind == "UR")
                        if i == 0:
                            pe.wait_ge(mhi_done.sem, mhi_done.at(it, (b, l, (side + 1) * NC - 1)))
                            pe.wait_ge(mlo_done.sem, mlo_done.at(it, (b, l, (side + 1) * NC - 1)))
                        cols = slice(i * P, (i + 1) * P)
                        to = slice(0, max((i + 1) * P, MIN_COLS)) if side == 0 else slice(min(i * P, S - MIN_COLS), S)
                        dst = open_bank(job, it, last)
                        split_product(dst[:, to], [(mhi[:, side * NC + c, cols], mlo[:, side * NC + c, cols],
                                                    hthi[b][:, c, to], htlo[b][:, c, to])
                                                   for c in range(NC)]).then_inc(full[kind].sem, 1)
                    if kind == "D":
                        if i == 0:
                            pe.wait_ge(masked_done.sem, masked_done.at(it, (b, l, NT - 1)))
                            pe.wait_ge(upper_done.sem, upper_done.at(it, (b, l, NT - 1)))
                        if i == DIAG:
                            pe.wait_ge(lower_done.sem, lower_done.at(it, (b, l, NT - 1)))
                        dst = open_bank(job, it, last)
                        for t in range(NT):
                            src = lower[:, t, :] if i == DIAG else upper[:, t, :] if t == i else e[:, t, i * P:(i + 1) * P]
                            ins = pe.transpose(dst[:, t * P:(t + 1) * P], src, ident[:, :])
                        ins.then_inc(full["D"].sem, 1)
                    if kind == "C" and soft:
                        cols = slice(i * P, (i + 1) * P)
                        dst = open_bank(job, it, last)
                        pairs = [(j, j) for j in range(i, NT)] + [(DIAG, NT + i)] + [(j, NT + j) for j in range(i)]

                        def parts_ready(k):
                            a = pairs[k][0]
                            pe.wait_ge(dhi_done.sem, dhi_done.at(it, (b, l, a)))
                            pe.wait_ge(dlo_done.sem, dlo_done.at(it, (b, l, a)))
                            if k == 0:
                                pe.wait_ge(vhi_done.sem, vhi_done.at(it, (b, l, 2 * NT - 1)))
                                pe.wait_ge(vlo_done.sem, vlo_done.at(it, (b, l, 2 * NT - 1)))

                        split_product(dst[:, 0:D], [(athi[:, a, cols], atlo[:, a, cols], vhi[:, v, :], vlo[:, v, :])
                                                    for a, v in pairs], parts_ready if i == 0 else None).then_inc(full["C"].sem, 1)
                    if kind == "C" and not soft:
                        cols = slice(i * P, (i + 1) * P)
                        dst = open_bank(job, it, last)

                        def rows_ready(j):
                            pe.wait_ge(ahi_done.sem, ahi_done.at(it, (b, l, j)))
                            pe.wait_ge(alo_done.sem, alo_done.at(it, (b, l, j)))
                            pe.wait_ge(vhi_done.sem, vhi_done.at(it, (b, l, j)))
                            pe.wait_ge(vlo_done.sem, vlo_done.at(it, (b, l, j)))

                        split_product(dst[:, 0:DX], [(athi[:, j, cols], atlo[:, j, cols], linhi[:, j, :], linlo[:, j, :])
                                                     for j in range(NT)], rows_ready if i == 0 else None).then_inc(full["C"].sem, 1)

            pe.wait_ge(masks_done, 3)
            pe.wait_ge(const_done, 3)
            turns(pe, run, [*full.values(), row1_done])

        def source_of(kind, b, l, i):
            return bank[bank_of[(kind, b, l, i)]]

        @block.scalar
        def _(act):
            def split_w(s, l, it):
                act.wait_ge(w_in[s].sem, w_in[s].at(it, l))
                act.activation(whi[:, s], wraw[:, s], ACT.Copy).then_inc(whi_done[s].sem, 1)

            def value_hi(b, l, i, it):
                dst = vhi[:, i, :] if l in SOFT else linhi[:, i, 0:D]
                act.wait_ge(biased_done.sem, biased_done.at(it, (b, l, i)))
                act.activation(dst, biased[:, biased_done.index[(b, l, i)] % RING, :], ACT.Copy).then_inc(vhi_done.sem, 1)

            def normalise_x(b, ph, it, last):
                act.wait_ge(xoff_done.sem, xoff_done.at(it, (b, ph)))
                if ph == 0:
                    if last is not None and b == 1:
                        act.wait_ge(relu_done.sem, relu_done.at(it - 1, (0, 0, NC - 1)))
                    if last is not None:
                        act.wait_ge(stored[b].sem, stored[b].at(it - b, "o"))
                for t in range(NT):
                    act.activation(n[:, t, :], xs[b][:, t, :], ACT.Identity, bias=xvec["off"][:, b, ph, t:t + 1],
                                   scale=xvec["root"][:, b, ph, t:t + 1]).then_inc(xnorm_done.sem, 1)

            def softmax_exp(b, l, t, it):
                act.wait_ge(nmax_done.sem, nmax_done.at(e_turn(it, b, l) if t == 0 else it, (b, l, t)))
                act.activation(e[:, t, :], source_of("U", b, l, t)[:, :], ACT.Exp, bias=vecs["nmax"][:, b, l, t:t + 1],
                               scale=SCALE, accum_out=vecs["esum"][:, b, l, t:t + 1]).then_inc(exp_done.sem, 1)

            def att_hi(b, l, t, it):
                act.wait_ge(weighted_done.sem, weighted_done.at(it, (b, l, t)))
                act.activation(athi[:, t, :], e[:, t, :], ACT.Copy).then_inc(ahi_done.sem, 1)

            def run(s, b, l, it, last):
                soft = l in SOFT
                beside = beside_of(s, b, l, last)
                if s == "Z" and not inlined(b, l, last):
                    normalise_x(b, l, it, last)
                if s == "T":
                    for c in range(NC):
                        act.wait_ge(full["T"].sem, full["T"].at(it, (b, l, c)))
                        act.wait_ge(hthi_done.sem, hthi_done.at(it, (b, l, c), HRING))
                        act.wait_ge(htlo_done.sem, htlo_done.at(it, (b, l, c), HRING))
                        if l % 2:
                            g = l // 2
                            act.activation(htf[:, relu_done.index[(b, l, c)] % HRING, :], source_of("T", b, l, c)[:, :], ACT.Relu, bias=gbt[:, g, 1, c:c + 1],
                                           scale=gbt[:, g, 0, c:c + 1]).then_inc(relu_done.sem, 1)
                        else:
                            act.activation(htf[:, relu_done.index[(b, l, c)] % HRING, :], source_of("T", b, l, c)[:, :], ACT.Relu).then_inc(relu_done.sem, 1)
                if s == "E" and not soft:
                    for i in range(2 * NC):
                        act.wait_ge(full["M"].sem, full["M"].at(it, (b, l, i)))
                        act.activation(mhi[:, i, :], source_of("M", b, l, i)[:, :], ACT.Copy).then_inc(mhi_done.sem, 1)
                if s == "E" and soft:
                    act.wait_ge(alo_done.sem, alo_done.at(it if (b, l) == (0, 0) else it - 1, (1, 3, NT - 1)))
                    act.wait_ge(full["U"].sem, full["U"].at(it, (b, l, 0)))
                    act.activation(upper[:, 0:NT - 1, :], source_of("U", b, l, 0)[:, P:S].rearrange("p (j q) -> p j q", q=P),
                                   ACT.Copy).then_inc(above_done.sem, 1)
                    act.wait_ge(row1_done.sem, row1_done.at(it, (b, l, 0)))
                    act.activation(lower[:, 0:NT - 2, :], source_of("U", b, l, 1)[:, 2 * P:S].rearrange("p (j q) -> p j q", q=P),
                                   ACT.Copy).then_inc(above_done.sem, 1)
                if s == "F" and soft:
                    act.wait_ge(diag_done.sem, diag_done.at(it, (b, l, 0), 1))
                    for t in range(NT):
                        softmax_exp(b, l, t, it)
                    for i in range(2 * NT):
                        if i == 2 * NT - 1 and beside:
                            normalise_x(*beside, it, last)
                        value_hi(b, l, i, it)
                if s == "F" and not soft:
                    value_hi(b, l, 0, it)
                    for t in range(NT):
                        if t == NT - 1 and beside:
                            normalise_x(*beside, it, last)
                        act.wait_ge(scores_done.sem, scores_done.at(it, (b, l, t)))
                        act.activation(e[:, t, :], e[:, t, :], ACT.Exp, scale=SCALE).then_inc(exp_done.sem, 1)
                        if t > 0:
                            att_hi(b, l, t - 1, it)
                if s == "H" and not soft:
                    value_hi(b, l, 1, it)
                    att_hi(b, l, NT - 1, it)
                    for t in range(2, NT):
                        value_hi(b, l, t, it)
                if s == "D" and soft:
                    for i in range(NT + 1):
                        act.wait_ge(full["D"].sem, full["D"].at(it, (b, l, i)))
                        act.activation(athi[:, i, :], source_of("D", b, l, i)[:, :], ACT.Copy).then_inc(dhi_done.sem, 1)
                if s == "K":
                    if b == 1:
                        k, i = ("HS", NT - 1) if soft else ("V", NT - 1)
                        act.wait_ge(full[k].sem, full[k].at(it, (b, l, i)))
                        for w in range(3):
                            split_w(w, (l + 1) % LAYERS, it)
                    if last and (b, l) == (1, 3):
                        act.wait_ge(stored[0].sem, stored[0].at(it, "o"))
                    if not soft:
                        for t in range(NT):
                            act.wait_ge(rrec_done.sem, rrec_done.at(it, (b, l, t)))
                            act.activation(n[:, t, :], source_of("C", b, l, t)[:, 0:D], ACT.Copy,
                                           scale=vecs["rec"][:, b, l, t:t + 1]).then_inc(ectx_done.sem, 1)
                if s == "L":
                    act.wait_ge(off_done.sem, off_done.at(it, (b, l, 0)))
                    for t in range(NT):
                        act.activation(n[:, t, :], n[:, t, :], ACT.Identity, bias=vecs["off"][:, b, l, t:t + 1],
                                       scale=vecs["rs"][:, b, l, t:t + 1]).then_inc(norm_done.sem, 1)

            act.wait_ge(gbt_in, 16)
            turns(act, run, [relu_done, above_done, exp_done, vhi_done, dhi_done, mhi_done, ahi_done, ectx_done, norm_done, xnorm_done, *whi_done], split_w)

        @block.vector
        def _(dve):
            def add_bias(b, l, i, it):
                slot = i // NT if l in SOFT else 2
                dve.wait_ge(full["V"].sem, full["V"].at(it, (b, l, i)))
                if i % NT == 0:
                    dve.wait_ge(bias_in[slot].sem, bias_in[slot].at(w_turn(it, l), l))
                dve.wait_ge(vhi_done.sem, vhi_done.at(it, (b, l, i), RING))
                dve.wait_ge(vlo_done.sem, vlo_done.at(it, (b, l, i), RING))
                dve.tensor_tensor(biased[:, biased_done.index[(b, l, i)] % RING, :], source_of("V", b, l, i)[:, 0:D],
                                  bias[:, slot, :], ALU.add).then_inc(biased_done.sem, 1)

            def att_lo(b, l, t, it):
                dve.wait_ge(ahi_done.sem, ahi_done.at(it, (b, l, t)))
                dve.tensor_tensor(atlo[:, t, :], e[:, t, :], athi[:, t, :].bitcast(F32), ALU.subtract).then_inc(alo_done.sem, 1)

            def weigh(b, l, t, it):
                dve.wait_ge(exp_done.sem, exp_done.at(it, (b, l, t)))
                dve.tensor_tensor(e[:, t, :], e[:, t, :], adjt[b][:, t, :], ALU.mult).then_inc(weighted_done.sem, 1)

            def stats_x(b, ph, t, it):
                if ph == 0 and t % (NT // 2) == 0:
                    h = t // (NT // 2)
                    dve.wait_ge(x_in[b][h].sem, x_in[b][h].at(it - b, "x"))
                if ph == 1:
                    dve.wait_ge(resid_done.sem, resid_done.at(it, (b, 1, t)))
                dve.bn_stats(stats[:, t, :], xs[b][:, t, :]).then_inc(xstats_done.sem, 1)

            def aggregate_x(b, ph, it):
                dve.wait_ge(xstats_done.sem, xstats_done.at(it, (b, ph, NT - 1)))
                dve.tensor_copy(carrier[:, :], stats[:, NT - 1, 0:1])
                for t in range(NT):
                    dve.bn_aggr(xmv[:, b, ph, t, :], stats[:, t, :]).then_inc(xaggr_done.sem, 1)
                dve.wait_ge(xaggr_done.sem, xaggr_done.at(it, (b, ph, NT - 1)))
                dve.tensor_scalar(xvec["va"][:, b, ph, :], xmv[:, b, ph, :, 1], NORM_EPS, None, ALU.add).then_inc(xva_done.sem, 1)

            def row_max(b, l, t, it):
                dve.wait_ge(full["U"].sem, full["U"].at(it, (b, l, t)))
                dve.tensor_reduce(vecs["rmax"][:, b, l, t:t + 1], source_of("U", b, l, t)[:, :], AX_X, ALU.max).then_inc(max_done.sem, 1)
                dve.wait_ge(max_done.sem, max_done.at(it, (b, l, t)))
                dve.tensor_scalar(vecs["nmax"][:, b, l, t:t + 1], vecs["rmax"][:, b, l, t:t + 1], -SCALE, None,
                                  ALU.mult).then_inc(nmax_done.sem, 1)

            def diagonal_parts(b, l, t, it):
                block_ = e[:, t, t * P:(t + 1) * P]
                dve.wait_ge(masked_done.sem, masked_done.at(it, (b, l, t)))
                dve.wait_ge(diag_done.sem, diag_done.at(it, (b, l, t), 1))
                dve.tensor_tensor_reduce(diag_scratch[:, :], block_, ident[:, :], 1.0, 0.0, ALU.mult, ALU.add,
                                         vecs["diag"][:, b, l, t:t + 1]).then_inc(diag_done.sem, 1)
                dve.tensor_tensor(lower[:, t, :], block_, m_lo[:, :], ALU.mult).then_inc(lower_done.sem, 1)

            def offset_x(b, ph, it):
                dve.wait_ge(xroot_done.sem, xroot_done.at(it, (b, ph)))
                dve.scalar_tensor_tensor(out=xvec["off"][:, b, ph, :], in0=xmv[:, b, ph, :, 0], scalar=-1.0,
                                         in1=xvec["root"][:, b, ph, :], op0=ALU.mult, op1=ALU.mult).then_inc(xoff_done.sem, 1)

            def run(s, b, l, it, last):
                soft = l in SOFT
                v = {k: t[:, b, l, :] for k, t in vecs.items()}
                beside = beside_of(s, b, l, last)
                if s in "XN":
                    ph = 0 if s == "X" else 1
                    if not inlined(b, ph, last):
                        for t in range(NT):
                            stats_x(b, ph, t, it)
                        aggregate_x(b, ph, it)
                if s == "T":
                    for c in range(NC):
                        dve.wait_ge(relu_done.sem, relu_done.at(it, (b, l, c)))
                        dve.tensor_copy(hthi[b][:, c, :], htf[:, relu_done.index[(b, l, c)] % HRING, :]).then_inc(hthi_done.sem, 1)
                if s == "E" and soft:
                    dve.wait_ge(above_done.sem, above_done.at(it, (b, l, 0)))
                    row_max(b, l, 0, it)
                if s == "E" and not soft:
                    for i in range(2 * NC):
                        dve.wait_ge(mhi_done.sem, mhi_done.at(it, (b, l, i)))
                        dve.tensor_tensor(mlo[:, i, :], source_of("M", b, l, i)[:, :], mhi[:, i, :].bitcast(F32),
                                          ALU.subtract).then_inc(mlo_done.sem, 1)
                if s == "F" and soft:
                    if l == 0:
                        dve.wait_ge(adj_in[b].sem, adj_in[b].at(it - 1, "a"))
                    for t in range(1, NT):
                        row_max(b, l, t, it)
                    for i in range(2 * NT):
                        add_bias(b, l, i, it)
                        if i < NT:
                            dve.wait_ge(exp_done.sem, exp_done.at(it, (b, l, i)))
                            dve.tensor_tensor_reduce(e[:, i, :], e[:, i, :], adjs[b][:, i, :], 1.0, 0.0, ALU.mult, ALU.add,
                                                     v["dsum"][:, i:i + 1]).then_inc(masked_done.sem, 1)
                        if beside:
                            for tile in {NT - 1: (0, 1), NT: (2,), NT + 1: (3,)}.get(i, ()):
                                stats_x(*beside, tile, it)
                            if i == NT + 1:
                                aggregate_x(*beside, it)
                        if i >= NT:
                            diagonal_parts(b, l, i - NT, it)
                        if beside and i == NT + 2:
                            offset_x(*beside, it)
                if s == "F" and not soft:
                    add_bias(b, l, 0, it)
                    if l == 2:
                        dve.wait_ge(adjr_done.sem, adjr_done.at(it, (b, l, 0)))
                    dve.wait_ge(adjl2_done.sem, adjl2_done.at(it, (b, l, 0)))
                    for t in range(NT):
                        lo = t * P
                        dve.wait_ge(full["UL"].sem, full["UL"].at(it, (b, l, t)))
                        if t == 0:
                            dve.wait_ge(ahi_done.sem, ahi_done.at(it, (b, l, 0), 1))
                        if t > 0:
                            dve.tensor_tensor(e[:, t, 0:lo], source_of("UL", b, l, t)[:, 0:lo], adjt[b][:, t, 0:lo], ALU.mult)
                        dve.tensor_tensor(lower[:, t, :], source_of("UL", b, l, t)[:, lo:lo + P], upper[:, t, :],
                                          ALU.mult).then_inc(left_done.sem, 1)
                        dve.wait_ge(full["UR"].sem, full["UR"].at(it, (b, l, t)))
                        dve.tensor_tensor(e[:, t, lo:S], source_of("UR", b, l, t)[:, lo:S], adjs[b][:, t, lo:S],
                                          ALU.mult).then_inc(right_done.sem, 1)
                        if t >= 1:
                            weigh(b, l, t - 1, it)
                        if t >= 2:
                            att_lo(b, l, t - 2, it)
                        if beside and t < 2:
                            for tile in range(NT)[HALVES[t]]:
                                stats_x(*beside, tile, it)
                            if t == 1:
                                aggregate_x(*beside, it)
                        if beside and t == 2:
                            offset_x(*beside, it)
                if s == "H" and soft:
                    dve.wait_ge(bias_in[2].sem, bias_in[2].at(w_turn(it, l), l))
                    for t in range(NT):
                        dve.wait_ge(full["HS"].sem, full["HS"].at(it, (b, l, t)))
                        dve.tensor_tensor(hs[:, t, :], source_of("HS", b, l, t)[:, 0:D], bias[:, 2, :], ALU.add).then_inc(hs_done.sem, 1)
                    dve.scalar_tensor_tensor(out=v["den"], in0=v["esum"], scalar=ATT_EPS, in1=v["dsum"],
                                             op0=ALU.mult, op1=ALU.add).then_inc(den_done.sem, 1)
                    dve.wait_ge(den_done.sem, den_done.at(it, (b, l, 0)))
                    dve.reciprocal(v["rec"], v["den"]).then_inc(rec_done.sem, 1)
                    dve.wait_ge(rec_done.sem, rec_done.at(it, (b, l, 0)))
                    dve.tensor_tensor(v["rec2"], v["rec"], v["rec"], ALU.mult).then_inc(rec2_done.sem, 1)
                if s == "H" and not soft:
                    add_bias(b, l, 1, it)
                    weigh(b, l, NT - 1, it)
                    att_lo(b, l, NT - 2, it)
                    add_bias(b, l, 2, it)
                    att_lo(b, l, NT - 1, it)
                    add_bias(b, l, 3, it)
                if s == "D" and soft:
                    for i in range(NT + 1):
                        dve.wait_ge(dhi_done.sem, dhi_done.at(it, (b, l, i)))
                        dve.tensor_tensor(atlo[:, i, :], source_of("D", b, l, i)[:, :], athi[:, i, :].bitcast(F32),
                                          ALU.subtract).then_inc(dlo_done.sem, 1)
                if s == "K":
                    if soft:
                        dve.wait_ge(hs_done.sem, hs_done.at(it, (b, l, NT - 1)))
                        dve.wait_ge(diag_done.sem, diag_done.at(it, (b, l, NT - 1)))
                    for t in range(NT):
                        dve.wait_ge(full["C"].sem, full["C"].at(it, (b, l, t)))
                        if soft:
                            dve.scalar_tensor_tensor(out=n[:, t, :], in0=hs[:, t, :], scalar=v["diag"][:, t:t + 1],
                                                     in1=source_of("C", b, l, t)[:, 0:D], op0=ALU.mult, op1=ALU.add).then_inc(ctx_done.sem, 1)
                            dve.wait_ge(ctx_done.sem, ctx_done.at(it, (b, l, t)))
                        else:
                            dve.tensor_scalar(v["den"][:, t:t + 1], source_of("C", b, l, t)[:, D:D + 1], ATT_EPS, None,
                                              ALU.add).then_inc(rsum_done.sem, 1)
                            dve.wait_ge(rsum_done.sem, rsum_done.at(it, (b, l, t)))
                            dve.reciprocal(v["rec"][:, t:t + 1], v["den"][:, t:t + 1]).then_inc(rrec_done.sem, 1)
                            dve.wait_ge(ectx_done.sem, ectx_done.at(it, (b, l, t)))
                        dve.bn_stats(stats[:, t, :], n[:, t, :]).then_inc(stats_done.sem, 1)
                    dve.wait_ge(stats_done.sem, stats_done.at(it, (b, l, NT - 1)))
                    dve.tensor_copy(carrier[:, :], stats[:, NT - 1, 0:1])
                    for t in range(NT):
                        dve.bn_aggr(mv[:, b, l, t, :], stats[:, t, :]).then_inc(aggr_done.sem, 1)
                    dve.wait_ge(aggr_done.sem, aggr_done.at(it, (b, l, NT - 1)))
                    mean, var = mv[:, b, l, :, 0], mv[:, b, l, :, 1]
                    if soft:
                        dve.tensor_tensor(v["va"], var, v["rec2"], ALU.mult).then_inc(va_done.sem, 1)
                        dve.wait_ge(va_done.sem, va_done.at(it, (b, l, 0)))
                        dve.tensor_scalar(v["vb"], v["va"], SOFT_EPS, None, ALU.add).then_inc(vb_done.sem, 1)
                        dve.wait_ge(root_done.sem, root_done.at(it, (b, l, 0)))
                        dve.tensor_tensor(v["rs"], v["root"], v["rec"], ALU.mult).then_inc(rs_done.sem, 1)
                    else:
                        dve.tensor_scalar(v["va"], var, float(D) / (D - 1), None, ALU.mult).then_inc(va_done.sem, 1)
                        dve.wait_ge(root_done.sem, root_done.at(it, (b, l, 0)))
                        dve.tensor_scalar(v["vb"], v["root"], EXP_EPS, None, ALU.add).then_inc(eps_done.sem, 1)
                        dve.wait_ge(eps_done.sem, eps_done.at(it, (b, l, 0)))
                        dve.reciprocal(v["rs"], v["vb"]).then_inc(rs_done.sem, 1)
                    dve.wait_ge(rs_done.sem, rs_done.at(it, (b, l, 0)))
                    dve.scalar_tensor_tensor(out=v["off"], in0=mean, scalar=-1.0, in1=v["rs"],
                                             op0=ALU.mult, op1=ALU.mult).then_inc(off_done.sem, 1)
                if s == "R":
                    dve.wait_ge(gb_in.sem, gb_in.at(it, l))
                    for t in range(NT):
                        dve.wait_ge(norm_done.sem, norm_done.at(it, (b, l, t)))
                        dve.tensor_tensor(n[:, t, :], n[:, t, :], gb[:, 0, :], ALU.mult).then_inc(gain_done.sem, 1)
                    for t in range(NT):
                        dve.wait_ge(affine_done.sem, affine_done.at(it, (b, l, t)))
                        dst = xs[b] if l == 1 else n
                        dve.scalar_tensor_tensor(out=dst[:, t, :], in0=n[:, t, :], scalar=0.0, in1=xs[b][:, t, :],
                                                 op0=ALU.max, op1=ALU.add).then_inc(resid_done.sem, 1)
                if s == "Z" and not inlined(b, l, last):
                    offset_x(b, l, it)

            dve.memset(half[:, 0, :], 0.5).then_inc(const_done, 1)
            dve.memset(half[:, 1, :], -0.5).then_inc(const_done, 1)
            dve.memset(linhi[:, :, D:DX].bitcast(F32), 1.0).then_inc(const_done, 1)
            dve.memset(linlo[:, :, D:DX].bitcast(F32), 0.0).then_inc(const_done, 1)
            dve.wait_ge(masks_done, 3)
            turns(dve, run, [hthi_done, max_done, nmax_done, masked_done, diag_done, lower_done, den_done, rec_done, rec2_done, biased_done,
                             hs_done, dlo_done, mlo_done, right_done, left_done, weighted_done, gain_done, alo_done, rsum_done, rrec_done, ctx_done,
                             stats_done, aggr_done, va_done, vb_done, eps_done, rs_done, off_done, resid_done,
                             xstats_done, xaggr_done, xva_done, xoff_done])

        @block.gpsimd
        def _(pool):
            def split_w(s, l, it):
                pool.wait_ge(whi_done[s].sem, whi_done[s].at(it, l))
                pool.tensor_tensor(wlo[:, s], wraw[:, s], whi[:, s].bitcast(F32), ALU.subtract).then_inc(wlo_done[s].sem, 1)

            def value_lo(b, l, i, it):
                hi, dst = (vhi[:, i, :], vlo[:, i, :]) if l in SOFT else (linhi[:, i, 0:D], linlo[:, i, 0:D])
                pool.wait_ge(vhi_done.sem, vhi_done.at(it, (b, l, i)))
                pool.tensor_tensor(dst, biased[:, biased_done.index[(b, l, i)] % RING, :], hi.bitcast(F32),
                                   ALU.subtract).then_inc(vlo_done.sem, 1)

            def root_x(b, ph, it):
                pool.wait_ge(xva_done.sem, xva_done.at(it, (b, ph)))
                pool.tensor_tensor(xvec["root"][:, b, ph, :], xvec["va"][:, b, ph, :], half[:, 1, :],
                                   ALU.pow).then_inc(xroot_done.sem, 1)

            def diagonal(a):
                v = a[:, :, :].rearrange("p t s -> p (t s)")
                return [v[:, t * (S + P):t * (S + P) + P] for t in range(NT)]

            def run(s, b, l, it, last):
                soft = l in SOFT
                beside = beside_of(s, b, l, last)
                if s == "T":
                    for c in range(NC):
                        pool.wait_ge(hthi_done.sem, hthi_done.at(it, (b, l, c)))
                        pool.tensor_tensor(htlo[b][:, c, :], htf[:, relu_done.index[(b, l, c)] % HRING, :], hthi[b][:, c, :].bitcast(F32),
                                           ALU.subtract).then_inc(htlo_done.sem, 1)
                if s == "F" and soft:
                    for i in range(2 * NT):
                        if i == 2 * NT - 2 and beside:
                            root_x(*beside, it)
                        value_lo(b, l, i, it)
                        if i < NT:
                            pool.wait_ge(masked_done.sem, masked_done.at(it, (b, l, i)))
                            pool.tensor_tensor(upper[:, i, :], diagonal(e)[i], m_up[:, :], ALU.mult).then_inc(upper_done.sem, 1)
                if s == "E" and not soft:
                    if l == 2:
                        pool.wait_ge(masked_done.sem, masked_done.at(it, (b, 1, NT - 1)))
                        for blk in diagonal(adjs[b]):
                            ins = pool.tensor_tensor(blk, blk, m_up[:, :], ALU.mult)
                        ins.then_inc(adjr_done.sem, 1)
                        pool.wait_ge(adjt_in[b].sem, adjt_in[b].at(it - 1, "a"))
                    pool.wait_ge(left_done.sem, left_done.at(it, (b, l, 0), 1))
                    if l == 2 and b == 0:
                        pool.wait_ge(full["D"].sem, full["D"].at(it, (1, 1, NT)))
                    for t, blk in enumerate(diagonal(adjt[b])):
                        ins = pool.tensor_tensor(upper[:, t, :], blk, m_up[:, :], ALU.mult)
                    ins.then_inc(adjl_done.sem, 1)
                    pool.wait_ge(adjl_done.sem, adjl_done.at(it, (b, l, 0)))
                    for t, blk in enumerate(diagonal(adjt[b])):
                        ins = pool.tensor_tensor(upper[:, t, :], blk, upper[:, t, :], ALU.subtract)
                    ins.then_inc(adjl2_done.sem, 1)
                if s == "F" and not soft:
                    for t in range(NT):
                        if t == 2 and beside:
                            root_x(*beside, it)
                        blk = diagonal(e)[t]
                        pool.wait_ge(right_done.sem, right_done.at(it, (b, l, t)))
                        pool.tensor_tensor(blk, blk, lower[:, t, :], ALU.add).then_inc(scores_done.sem, 1)
                        if t == 0:
                            value_lo(b, l, 0, it)
                if s == "H" and not soft:
                    for t in range(1, NT):
                        value_lo(b, l, t, it)
                if s == "K":
                    if b == 1:
                        split_w(0, (l + 1) % LAYERS, it)
                        split_w(1, (l + 1) % LAYERS, it)
                        split_w(2, (l + 1) % LAYERS, it)
                    src = vb_done if soft else va_done
                    pool.wait_ge(src.sem, src.at(it, (b, l, 0)))
                    pool.tensor_tensor(vecs["root"][:, b, l, :], vecs["vb" if soft else "va"][:, b, l, :],
                                       half[:, 1 if soft else 0, :], ALU.pow).then_inc(root_done.sem, 1)
                if s == "R":
                    pool.wait_ge(gb_in.sem, gb_in.at(it, l))
                    for t in range(NT):
                        pool.wait_ge(gain_done.sem, gain_done.at(it, (b, l, t)))
                        pool.tensor_tensor(n[:, t, :], n[:, t, :], gb[:, 1, :], ALU.add).then_inc(affine_done.sem, 1)
                if s in "XN" and not inlined(b, 0 if s == "X" else 1, last):
                    root_x(b, 0 if s == "X" else 1, it)

            for m in (ident, m_up, m_lo):
                pool.memset(m[:, :], 1.0).then_inc(mask_step, 1)
            pool.wait_ge(mask_step, 3)
            for m, op, sign in ((ident, ALU.is_equal, 1), (m_up, ALU.is_gt, 1), (m_lo, ALU.is_gt, -1)):
                pool.affine_select(out=m[:, :], in_=m[:, :], compare_op=op, fill=0.0, base=0,
                                   pattern=[[sign, P]], channel_multiplier=-sign).then_inc(masks_done, 1)
            pool.wait_ge(masks_done, 3)
            pool.wait_ge(const_done, 4)
            turns(pool, run, [htlo_done, upper_done, vlo_done, adjr_done, adjl_done, adjl2_done, scores_done,
                              root_done, affine_done, xroot_done, *wlo_done], split_w)


_NAMES = ["L0_gnn_Wl", "L0_gnn_bl", "L0_gnn_Ws", "L0_gnn_bs", "L0_gnn_Wr", "L0_gnn_br", "L0_gnn_ln_w", "L0_gnn_ln_b",
          "L1_gnn_W_left", "L1_gnn_W_right", "L1_gnn_W_lin", "L1_gnn_b_lin", "L1_gnn_ln_a", "L1_gnn_ln_b"]


def kernel(**inputs):
    import numpy as _np
    import concourse.bacc as _bacc
    from concourse import mybir as _mybir
    from concourse.bass_utils import run_bass_kernel_spmd as _run

    nc = _bacc.Bacc("TRN2", target_bir_lowering=False, num_devices=1)
    arrays, args = {}, []

    def give(name, a):
        a = _np.ascontiguousarray(a)
        arrays[f"in_{name}_dram"] = a
        args.append(nc.dram_tensor(f"in_{name}_dram", a.shape, _mybir.dt.from_np(a.dtype), kind="ExternalInput").ap())

    x = _np.asarray(inputs["x"])
    adj = _np.asarray(inputs["adj"])
    give("x", x)
    give("adj", adj)
    give("adj_t", adj.transpose(0, 2, 1))
    for name in _NAMES:
        a = _np.asarray(inputs[name])
        give(name, a.transpose(0, 2, 1) if a.ndim == 3 else a)
    norms = _np.stack([_np.asarray(inputs[k])[0] for k in ("L0_gnn_ln_w", "L0_gnn_ln_b", "L1_gnn_ln_a", "L1_gnn_ln_b")])
    give("norm_t", norms.reshape(2, 2, -1, P).transpose(3, 0, 1, 2))
    out = nc.dram_tensor("out_0_dram", x.shape, _mybir.dt.float32, kind="ExternalOutput").ap()
    program(nc, *args, out)
    r = _run(nc, [arrays], core_ids=[0])
    return r.results[0]["out_0_dram"]
```
